# Optimizing a Trainium2 kernel written in Bass

```python
import numpy as np
import jax
import jax.numpy as jnp

def _softmax(x, axis=-1):
    return jax.nn.softmax(x, axis=axis)

def _gelu(x):
    return jax.nn.gelu(x, approximate=True)

def _silu(x):
    return jax.nn.silu(x)

def _sigmoid(x):
    return jax.nn.sigmoid(x)

def _layernorm(x, axis=-1, eps=1e-05):
    m = jnp.mean(x, axis=axis, keepdims=True)
    v = jnp.var(x, axis=axis, keepdims=True)
    return (x - m) / jnp.sqrt(v + eps)

def _scatter_add(tgt, idx, src, axis=0):
    return tgt.at[idx].add(src)

def _segment_sum(src, seg, n):
    return jax.ops.segment_sum(src, seg, n)
kernel_name = 'mk_conv_seq_d2_conv_nhwc512_r4_f7cdb4'

def setup_inputs(seed: int=0):
    np.random.seed(seed)
    _w = jnp.asarray

    def _rec_inputs():
        import jax
        import jax.numpy as jnp
        _gk = jax.random.key(seed)
        x = 7.22e-05 + 1 * jax.random.normal(jax.random.fold_in(_gk, 1), (4, 16, 16, 128), jnp.float32)
        return x
    x = _rec_inputs()

    def _L0_conv_setup():
        import jax, jax.numpy as jnp
        import numpy as np
        B, H, W, C = (4, 16, 16, 128)
        EPS = 0.001
        key = jax.random.key(seed)
        ks = jax.random.split(key, 16)
        c8, c2 = (C // 8, C // 2)
        sc = lambda fan_in: 1.0 / np.sqrt(fan_in)
        inp = {'x': jax.random.normal(ks[0], (B, H, W, C), dtype=jnp.float32), 'wf': jax.random.normal(ks[1], (C, c8), dtype=jnp.float32) * sc(C), 'bf': jnp.zeros((c8,), jnp.float32), 'wg': jax.random.normal(ks[2], (C, c8), dtype=jnp.float32) * sc(C), 'bg': jnp.zeros((c8,), jnp.float32), 'wh': jax.random.normal(ks[3], (C, c2), dtype=jnp.float32) * sc(C), 'bh': jnp.zeros((c2,), jnp.float32), 'wo': jax.random.normal(ks[4], (c2, C), dtype=jnp.float32) * sc(c2), 'bo': jnp.zeros((C,), jnp.float32), 'gamma': jax.random.normal(ks[5], (1,), dtype=jnp.float32) * 0.05, 'wc': jax.random.normal(ks[6], (2 * C, C), dtype=jnp.float32) * sc(2 * C), 'bc': jnp.zeros((C,), jnp.float32), 'bn_scale': jnp.ones((C,), jnp.float32), 'bn_bias': jnp.zeros((C,), jnp.float32), 'bn_mean': jnp.zeros((C,), jnp.float32), 'bn_var': jnp.ones((C,), jnp.float32)}
        return inp
    _L0_conv_all = _L0_conv_setup()
    _L0_conv_in = {k: v for k, v in _L0_conv_all.items() if k in ('wf', 'bf', 'wg', 'bg', 'wh', 'bh', 'wo', 'bo', 'gamma', 'wc', 'bc', 'bn_scale', 'bn_bias', 'bn_mean', 'bn_var')}
    del _L0_conv_all

    def _L1_conv_setup():
        import jax, jax.numpy as jnp
        import numpy as np
        B, H, W, C = (4, 16, 16, 128)
        LN_EPS = 0.001
        key = jax.random.key(seed)
        ks = jax.random.split(key, 10)
        s = 1.0 / np.sqrt(C)
        return {'x': jax.random.normal(ks[0], (B, H, W, C), dtype=jnp.float32), 'ln_g': jnp.ones((C,), jnp.float32), 'ln_b': jnp.zeros((C,), jnp.float32), 'Wq': jax.random.normal(ks[1], (C, C), jnp.float32) * s, 'bq': jnp.zeros((C,), jnp.float32), 'Wk': jax.random.normal(ks[2], (C, C), jnp.float32) * s, 'bk': jnp.zeros((C,), jnp.float32), 'Wv': jax.random.normal(ks[3], (C, C), jnp.float32) * s, 'bv': jnp.zeros((C,), jnp.float32), 'Wp': jax.random.normal(ks[4], (C, C), jnp.float32) * s, 'bp': jnp.zeros((C,), jnp.float32)}
    _L1_conv_all = _L1_conv_setup()
    _L1_conv_in = {k: v for k, v in _L1_conv_all.items() if k in ('ln_g', 'ln_b', 'Wq', 'bq', 'Wk', 'bk', 'Wv', 'bv', 'Wp', 'bp')}
    del _L1_conv_all
    return {'x': x, 'L0_conv_wf': _L0_conv_in['wf'], 'L0_conv_bf': _L0_conv_in['bf'], 'L0_conv_wg': _L0_conv_in['wg'], 'L0_conv_bg': _L0_conv_in['bg'], 'L0_conv_wh': _L0_conv_in['wh'], 'L0_conv_bh': _L0_conv_in['bh'], 'L0_conv_wo': _L0_conv_in['wo'], 'L0_conv_bo': _L0_conv_in['bo'], 'L0_conv_gamma': _L0_conv_in['gamma'], 'L0_conv_wc': _L0_conv_in['wc'], 'L0_conv_bc': _L0_conv_in['bc'], 'L0_conv_bn_scale': _L0_conv_in['bn_scale'], 'L0_conv_bn_bias': _L0_conv_in['bn_bias'], 'L0_conv_bn_mean': _L0_conv_in['bn_mean'], 'L0_conv_bn_var': _L0_conv_in['bn_var'], 'L1_conv_ln_g': _L1_conv_in['ln_g'], 'L1_conv_ln_b': _L1_conv_in['ln_b'], 'L1_conv_Wq': _L1_conv_in['Wq'], 'L1_conv_bq': _L1_conv_in['bq'], 'L1_conv_Wk': _L1_conv_in['Wk'], 'L1_conv_bk': _L1_conv_in['bk'], 'L1_conv_Wv': _L1_conv_in['Wv'], 'L1_conv_bv': _L1_conv_in['bv'], 'L1_conv_Wp': _L1_conv_in['Wp'], 'L1_conv_bp': _L1_conv_in['bp']}

def reference(x, L0_conv_wf, L0_conv_bf, L0_conv_wg, L0_conv_bg, L0_conv_wh, L0_conv_bh, L0_conv_wo, L0_conv_bo, L0_conv_gamma, L0_conv_wc, L0_conv_bc, L0_conv_bn_scale, L0_conv_bn_bias, L0_conv_bn_mean, L0_conv_bn_var, L1_conv_ln_g, L1_conv_ln_b, L1_conv_Wq, L1_conv_bq, L1_conv_Wk, L1_conv_bk, L1_conv_Wv, L1_conv_bv, L1_conv_Wp, L1_conv_bp):
    import jax
    import jax.numpy as jnp

    def _L0_conv_ref(x, wf, bf, wg, bg, wh, bh, wo, bo, gamma, wc, bc, bn_scale, bn_bias, bn_mean, bn_var):
        import jax, jax.numpy as jnp
        import numpy as np
        B, H, W, C = (4, 16, 16, 128)
        EPS = 0.001
        b, h, w, c = x.shape
        n = h * w
        xf = x.reshape(b, n, c)
        f = xf @ wf + bf
        g = xf @ wg + bg
        hv = xf @ wh + bh
        s = jnp.einsum('bnd,bmd->bnm', g, f)
        beta = jax.nn.softmax(s, axis=-1)
        o = jnp.einsum('bnm,bmd->bnd', beta, hv)
        o = o @ wo + bo
        att = gamma * o + xf
        cat = jnp.concatenate([att, xf], axis=-1)
        y = cat @ wc + bc
        y = (y - bn_mean) * (bn_scale / jnp.sqrt(bn_var + EPS)) + bn_bias
        y = jax.nn.relu(y)
        return y.reshape(b, h, w, c)

    def _L1_conv_ref(x, ln_g, ln_b, Wq, bq, Wk, bk, Wv, bv, Wp, bp):
        import jax, jax.numpy as jnp
        import numpy as np
        B, H, W, C = (4, 16, 16, 128)
        LN_EPS = 0.001
        b, h_, w_, c = x.shape
        n = h_ * w_
        mu = jnp.mean(x, axis=-1, keepdims=True)
        var = jnp.var(x, axis=-1, keepdims=True)
        hn = (x - mu) * jax.lax.rsqrt(var + LN_EPS) * ln_g + ln_b
        hf = hn.reshape(b, n, c)
        q = hf @ Wq + bq
        k = hf @ Wk + bk
        v = hf @ Wv + bv
        scale = 1.0 / jnp.sqrt(jnp.asarray(c, x.dtype))
        scores = jnp.einsum('bqc,bkc->bqk', q, k) * scale
        attn = jax.nn.softmax(scores, axis=-1)
        o = jnp.einsum('bqk,bkc->bqc', attn, v)
        o = o @ Wp + bp
        return x + o.reshape(b, h_, w_, c)

    def _gn(v, G=32, eps=1e-05):
        B_, H_, W_, C_ = v.shape
        g = v.reshape(B_, H_, W_, G, C_ // G)
        m = jnp.mean(g, axis=(1, 2, 4), keepdims=True)
        s = jnp.var(g, axis=(1, 2, 4), keepdims=True)
        return ((g - m) / jnp.sqrt(s + eps)).reshape(v.shape)

    def _ln_c(v, eps=1e-06):
        m = jnp.mean(v, axis=-1, keepdims=True)
        s = jnp.var(v, axis=-1, keepdims=True)
        return (v - m) / jnp.sqrt(s + eps)

    def _ln_t(v, eps=1e-05):
        m = jnp.mean(v, axis=-1, keepdims=True)
        s = jnp.var(v, axis=-1, keepdims=True)
        return (v - m) / jnp.sqrt(s + eps)

    def _to_tokens(v):
        B_, H_, W_, C_ = v.shape
        return v.reshape(B_, H_ * W_, C_)

    def _from_tokens(t, like):
        return t.reshape(like.shape)
    x = _L0_conv_ref(x, L0_conv_wf, L0_conv_bf, L0_conv_wg, L0_conv_bg, L0_conv_wh, L0_conv_bh, L0_conv_wo, L0_conv_bo, L0_conv_gamma, L0_conv_wc, L0_conv_bc, L0_conv_bn_scale, L0_conv_bn_bias, L0_conv_bn_mean, L0_conv_bn_var)
    x = _L1_conv_ref(x, L1_conv_ln_g, L1_conv_ln_b, L1_conv_Wq, L1_conv_bq, L1_conv_Wk, L1_conv_bk, L1_conv_Wv, L1_conv_bv, L1_conv_Wp, L1_conv_bp)
    return x

_drawn_inputs = setup_inputs


def setup_inputs(seed=0):
    import zlib

    import numpy as np

    out = dict(_drawn_inputs(seed))
    spreads = {'L0_conv_bf': (0.0, 2.0),
     'L0_conv_bg': (0.0, 0.8),
     'L0_conv_bh': (0.0, 0.8),
     'L0_conv_bo': (0.0, 2.0),
     'L0_conv_bc': (0.0, 0.1),
     'L0_conv_bn_scale': (1.0, 0.2),
     'L0_conv_bn_bias': (0.0, 0.1),
     'L0_conv_bn_mean': (0.0, 0.1),
     'L0_conv_bn_var': (1.0, 0.2),
     'L1_conv_ln_g': (1.0, 0.2),
     'L1_conv_ln_b': (0.0, 0.1),
     'L1_conv_bq': (0.0, 0.431),
     'L1_conv_bk': (0.0, 2.0),
     'L1_conv_bv': (0.0, 0.1),
     'L1_conv_bp': (0.0, 0.1)}
    factors = {'L0_conv_wf': 4.028, 'L0_conv_wg': 4.104, 'L0_conv_wh': 3.891, 'L0_conv_wo': 3.969}
    for name, (base, spread) in spreads.items():
        noise = np.random.default_rng([zlib.crc32(name.encode()), seed]).standard_normal(out[name].shape)
        drawn = base * np.exp(spread * noise) if base else spread * noise
        out[name] = jnp.asarray(drawn.astype(out[name].dtype))
    for name, factor in factors.items():
        out[name] = (out[name] * factor).astype(out[name].dtype)
    return out
```

```python
from contextlib import ExitStack

import concourse.bass as bass
from concourse import mybir

F32 = mybir.dt.float32
ALU = mybir.AluOpType
ACT = mybir.ActivationFunctionType
AX_X = mybir.AxisListType.X

P = 128
IMAGES = 4
TOKENS = 256
TILES = TOKENS // P
C = 128
CK = C // 8
CV = C // 2
BLOCK = 32
VW = C + 2
ATTENTIONS = 2 * IMAGES
BN_EPS = 1e-3
LN_EPS = 1e-3
SCORE_SCALE = float(C) ** -0.5

X0, FG_W, COLS = 0, IMAGES * TOKENS, IMAGES * TOKENS + 2 * BLOCK
COL_NAMES = ["bf", "bg", "gamma", "bo", "ln_g", "ln_b", "bq", "bk", "bv", "bp",
             "bn_var", "bn_scale", "bc", "bn_mean", "bn_bias"]
FIRST_W = COLS + len(COL_NAMES)
FOLD0 = ["wo", "wh_t", "bh", "wc_top", "wc_top_t", "wc_bottom_t", "identity"]
FOLD0_W = (len(FOLD0) - 1) * C + 1
FOLD1 = ["wv_t", "wp", "wq", "wk"]


PE_ORDER = """FG0 FOLD0 X0 S0 S1 X1 FOLD1 T0 X2 S2 M0 T1 X3 S3 M1 T2 H0 M2 T3 Q0 H1 V4 M3 S4 Q1 H2
              V5 T4 S5 Q2 H3 V6 M4 T5 S6 Q3 V7 M5 T6 S7 M6 T7 M7""".split()
ACT_ORDER = """FG0 FOLD0 V0 E0 E1 V1 FOLD1 P0 V2 E2 P1 V3 E3 P2 P3 Q0 V4 E4 Q1
               V5 P4 E5 Q2 V6 P5 E6 Q3 V7 P6 E7 P7""".split()
DVE_ORDER = """FG0 FOLD0 N0 N1 FOLD1 P0 N2 O0 P1 N3 O1 P2 L0 O2 P3 L1 H0 K0 O3 N4 L2 H1 K1
               P4 N5 L3 H2 K2 O4 P5 N6 H3 K3 O5 P6 N7 O6 P7 O7""".split()


def attention_blocks(nc, first, fold0, fold1, out):
    with ExitStack() as ctx:
        def sb(name, shape):
            return ctx.enter_context(nc.sbuf_tensor(name, shape, F32))

        def bank(name):
            return ctx.enter_context(nc.psum_tensor(name, [P, 512], F32))

        def sem(name):
            return ctx.enter_context(nc.semaphore(name))

        first_sb = sb("first_sb", [P, FIRST_W])
        fold0_sb = sb("fold0_sb", [P, FOLD0_W])
        fold1_sb = sb("fold1_sb", [P, len(FOLD1) * C])
        minus_half = sb("minus_half", [P, TILES])
        var_eps = sb("var_eps", [P, 1])
        power = sb("power", [P, 1])
        bn_a = sb("bn_a", [P, 1])
        gamma_a = sb("gamma_a", [P, 1])
        centre = sb("centre", [P, 1])
        shift = sb("shift", [P, 1])
        both_t = sb("both_t", [P, C])
        wh_wo_t = sb("wh_wo_t", [P, C + 1])
        w1_t = sb("w1_t", [P, C])
        w2_t = sb("w2_t", [P, C])
        const0_col = sb("const0_col", [P, 1])
        w1w2 = sb("w1w2", [P, 2 * C])
        const0 = sb("const0", [P, TILES, C])
        wvp = sb("wvp", [P, C])
        const1 = sb("const1", [P, TILES, C])
        f_all = sb("f_all", [P, TOKENS])
        g_all = sb("g_all", [P, TOKENS])
        values = sb("values", [P, ATTENTIONS, TILES, 2, VW])
        xw2 = sb("xw2", [P, IMAGES, TILES, C])
        neg_max = sb("neg_max", [P, ATTENTIONS, TILES])
        probs = sb("probs", [P, ATTENTIONS, TILES, TOKENS])
        probs_t = sb("probs_t", [P, ATTENTIONS, TILES, TOKENS])
        inv_sum = sb("inv_sum", [P, ATTENTIONS, TILES])
        pre = sb("pre", [P, IMAGES, TILES, C])
        y = sb("y", [P, IMAGES, TILES, C])
        y_const = sb("y_const", [P, IMAGES, TILES, C])
        stats = sb("stats", [P, IMAGES, TILES, 6])
        mean_var = sb("mean_var", [P, IMAGES, TILES, 2])
        ln_var = sb("ln_var", [P, IMAGES, TILES])
        rstd = sb("rstd", [P, IMAGES, TILES])
        normed = sb("normed", [P, IMAGES, TILES, C])
        h_t = sb("h_t", [P, IMAGES, TOKENS])
        q_t = sb("q_t", [P, IMAGES, TOKENS])
        bq_s = sb("bq_s", [P, 1])
        k_t = sb("k_t", [P, IMAGES, TOKENS])
        result = sb("result", [P, IMAGES, TILES, C])

        score_bank = [bank(f"score_bank{i}") for i in range(2)]
        turn_bank = [bank(f"turn_bank{t}") for t in range(TILES)]
        mix_bank = bank("mix_bank")
        value_bank = bank("value_bank")
        q_bank = bank("q_bank")
        k_bank = bank("k_bank")

        x_t = first_sb[:, X0:X0 + IMAGES * TOKENS]
        wf2 = first_sb[:, FG_W:FG_W + BLOCK]
        wg2 = first_sb[:, FG_W + BLOCK:FG_W + 2 * BLOCK]
        col = {n: first_sb[:, COLS + i:COLS + i + 1] for i, n in enumerate(COL_NAMES)}
        w, at = {}, 0
        for n in FOLD0:
            w[n] = fold0_sb[:, at:at + (1 if n == "bh" else C)]
            at += 1 if n == "bh" else C
        for i, n in enumerate(FOLD1):
            w[n] = fold1_sb[:, i * C:(i + 1) * C]
        wh_t_bh = fold0_sb[0:CV, C:2 * C + 1]
        identity = w["identity"]

        first_in, fold0_in, fold1_in = (sem(n) for n in ("first_in", "fold0_in", "fold1_in"))
        half_set = sem("half_set")
        ones_set = sem("ones_set")
        fg_made = sem("fg_made")
        f_ready = sem("f_ready")
        g_ready = sem("g_ready")
        bq_scaled = sem("bq_scaled")
        eps_added = sem("eps_added")
        powered = sem("powered")
        a_ready = sem("a_ready")
        gamma_a_ready = sem("gamma_a_ready")
        centred = sem("centred")
        shift_ready = sem("shift_ready")
        both_added = sem("both_added")
        wh_wo_made = sem("wh_wo_made")
        wh_wo_ready = sem("wh_wo_ready")
        w1_t_made = sem("w1_t_made")
        w1_t_ready = sem("w1_t_ready")
        w2_t_ready = sem("w2_t_ready")
        const0_col_ready = sem("const0_col_ready")
        w1w2_made = sem("w1w2_made")
        w1w2_ready = sem("w1w2_ready")
        const0_made = sem("const0_made")
        const0_ready = sem("const0_ready")
        wvp_made = sem("wvp_made")
        wvp_ready = sem("wvp_ready")
        const1_made = sem("const1_made")
        const1_ready = sem("const1_ready")
        scores_made = sem("scores_made")
        max_ready = sem("max_ready")
        probs_ready = sem("probs_ready")
        turned = sem("turned")
        turned0_ready = sem("turned0_ready")
        turned1_ready = sem("turned1_ready")
        xv_made = sem("xv_made")
        values_ready = sem("values_ready")
        xw2_ready = sem("xw2_ready")
        mixed = sem("mixed")
        inv_ready = sem("inv_ready")
        mix_read = sem("mix_read")
        relu_ready = sem("relu_ready")
        y_const_ready = sem("y_const_ready")
        stats_ready = sem("stats_ready")
        mean_ready = sem("mean_ready")
        ln_eps_added = sem("ln_eps_added")
        rstd_ready = sem("rstd_ready")
        normed_ready = sem("normed_ready")
        h_turned = sem("h_turned")
        h_ready = sem("h_ready")
        qk_made = sem("qk_made")
        q_ready = sem("q_ready")
        k_ready = sem("k_ready")
        stored = sem("stored")

        block = ctx.enter_context(nc.Block())

        @block.sync
        def _(sp):
            sp.dma_start(first_sb[:], first).then_inc(first_in, 16)
            sp.dma_start(fold1_sb[:], fold1).then_inc(fold1_in, 16)
            for b in range(IMAGES):
                sp.wait_ge(mix_read, TILES * (IMAGES + b + 1))
                sp.dma_start(out[b].rearrange("(t p) c -> p t c", p=P), result[:, b]).then_inc(stored, 16)
            sp.wait_ge(stored, 16 * IMAGES)

        def scores_of(j, t):
            return score_bank[j % 2][:, t * TOKENS:(t + 1) * TOKENS]

        @block.gpsimd
        def _(pool):
            pool.memset(minus_half[:], -0.5).then_inc(half_set, 1)
            pool.memset(values[:, :, :, 0, C:VW], 1.0).then_inc(ones_set, 1)
            pool.wait_ge(half_set, 1)
            pool.wait_ge(eps_added, 1)
            pool.tensor_tensor(out=power[:], in0=var_eps[:], in1=minus_half[:, 0:1], op=ALU.pow).then_inc(powered, 1)
            for b in range(IMAGES):
                if b == 0:
                    pool.wait_ge(const0_ready, TILES)
                pool.wait_ge(values_ready, b + 1)
                pool.tensor_tensor(out=xw2[:, b], in0=values[:, b, :, 1, 0:C], in1=const0[:], op=ALU.add).then_inc(xw2_ready, 1)
            for b in range(IMAGES):
                pool.wait_ge(ln_eps_added, b + 1)
                pool.tensor_tensor(out=rstd[:, b], in0=ln_var[:, b], in1=minus_half[:, 0:TILES],
                                   op=ALU.pow).then_inc(rstd_ready, 1)
                if b == 0:
                    pool.wait_ge(const1_ready, TILES)
                pool.wait_ge(relu_ready, b + 1)
                pool.tensor_tensor(out=y_const[:, b], in0=y[:, b], in1=const1[:], op=ALU.add).then_inc(y_const_ready, 1)

        @block.scalar
        def _(act):
            act.dma_start(fold0_sb[:], fold0).then_inc(fold0_in, 16)

            def take_g(_):
                act.wait_ge(first_in, 16)
                act.wait_ge(fg_made, 2)
                act.activation(g_all[:], k_bank[:, 0:TOKENS], ACT.Identity,
                               bias=col["bg"]).then_inc(g_ready, 1)

            def take_folds(n):
                if n == 0:
                    act.wait_ge(wh_wo_made, 1)
                    act.activation(wh_wo_t[:], mix_bank[:, 0:C + 1], ACT.Copy).then_inc(wh_wo_ready, 1)
                    act.wait_ge(w1w2_made, 1)
                    act.activation(w1w2[:], mix_bank[:, 0:2 * C], ACT.Copy).then_inc(w1w2_ready, 1)
                else:
                    act.wait_ge(wvp_made, 1)
                    act.activation(wvp[:], turn_bank[1][:, 0:C], ACT.Copy).then_inc(wvp_ready, 1)

            def exponentials(j):
                act.wait_ge(scores_made, TILES * (j + 1))
                act.wait_ge(max_ready, j + 1)
                for t in range(TILES):
                    act.activation(probs[:, j, t], scores_of(j, t), ACT.Exp,
                                   bias=neg_max[:, j, t:t + 1]).then_inc(probs_ready, 1)

            def take_values(j):
                act.wait_ge(xv_made, j + 1)
                act.wait_ge(ones_set, 1)
                kinds = 2 if j < IMAGES else 1
                made = value_bank[:, 0:TILES * kinds * C].rearrange("p (t k n) -> p t k n", t=TILES, k=kinds)
                act.activation(values[:, j, :, 0:kinds, 0:C], made, ACT.Copy).then_inc(values_ready, 1)

            def take_turned(j):
                act.wait_ge(turned, TILES * (j + 1))
                act.activation(probs_t[:, j, 1], turn_bank[1][:, 0:TOKENS], ACT.Copy).then_inc(turned1_ready, 1)

            def take_q(b):
                act.wait_ge(qk_made, 2 * b + 1)
                act.wait_ge(bq_scaled, 1)
                act.activation(q_t[:, b], q_bank[:, 0:TOKENS], ACT.Identity, bias=bq_s[:],
                               scale=SCORE_SCALE).then_inc(q_ready, 1)

            steps = {"FG": take_g, "FOLD": take_folds, "E": exponentials, "V": take_values,
                     "P": take_turned, "Q": take_q}
            for step in ACT_ORDER:
                steps[step[:-1]](int(step[-1]))

        @block.vector
        def _(dve):
            def take_f(_):
                dve.wait_ge(first_in, 16)
                dve.wait_ge(fg_made, 1)
                dve.tensor_scalar(f_all[:], q_bank[:, 0:TOKENS], col["bf"], None, ALU.add).then_inc(f_ready, 1)
                dve.tensor_scalar(bq_s[:], col["bq"], SCORE_SCALE, None, ALU.mult).then_inc(bq_scaled, 1)

            def folds(n):
                if n == 0:
                    dve.wait_ge(first_in, 16)
                    dve.tensor_scalar(var_eps[:], col["bn_var"], BN_EPS, None, ALU.add).then_inc(eps_added, 1)
                    dve.tensor_tensor(out=centre[:], in0=col["bc"], in1=col["bn_mean"], op=ALU.subtract).then_inc(centred, 1)
                    dve.wait_ge(fold0_in, 16)
                    dve.tensor_tensor(out=both_t[:], in0=w["wc_top_t"], in1=w["wc_bottom_t"],
                                      op=ALU.add).then_inc(both_added, 1)
                    dve.wait_ge(powered, 1)
                    dve.tensor_tensor(out=bn_a[:], in0=power[:], in1=col["bn_scale"], op=ALU.mult).then_inc(a_ready, 1)
                    dve.wait_ge(a_ready, 1)
                    dve.tensor_tensor(out=gamma_a[:], in0=bn_a[:], in1=col["gamma"], op=ALU.mult).then_inc(gamma_a_ready, 1)
                    dve.wait_ge(centred, 1)
                    dve.scalar_tensor_tensor(out=shift[:], in0=centre[:], scalar=bn_a[:], in1=col["bn_bias"],
                                             op0=ALU.mult, op1=ALU.add).then_inc(shift_ready, 1)
                    dve.wait_ge(both_added, 1)
                    dve.tensor_scalar(w2_t[:], both_t[:], bn_a[:], None, ALU.mult).then_inc(w2_t_ready, 1)
                    dve.wait_ge(gamma_a_ready, 1)
                    dve.wait_ge(w1_t_made, 1)
                    dve.tensor_scalar(w1_t[:], value_bank[:, 0:C], gamma_a[:], None, ALU.mult).then_inc(w1_t_ready, 1)
                    dve.wait_ge(shift_ready, 1)
                    dve.scalar_tensor_tensor(out=const0_col[:], in0=value_bank[:, C:C + 1], scalar=gamma_a[:],
                                             in1=shift[:], op0=ALU.mult, op1=ALU.add).then_inc(const0_col_ready, 1)
                    dve.wait_ge(const0_made, 1)
                    for t in range(TILES):
                        dve.tensor_copy(const0[:, t], turn_bank[0][:, 0:C]).then_inc(const0_ready, 1)
                else:
                    dve.wait_ge(const1_made, 1)
                    for t in range(TILES):
                        dve.tensor_copy(const1[:, t], mix_bank[:, 0:C]).then_inc(const1_ready, 1)

            def maxima(j):
                dve.wait_ge(scores_made, TILES * (j + 1))
                dve.tensor_reduce(neg_max[:, j], score_bank[j % 2][:].rearrange("p (t m) -> p t m", t=TILES),
                                  AX_X, ALU.max, negate=True).then_inc(max_ready, 1)

            def take_turned(j):
                dve.wait_ge(turned, TILES * j + 1)
                dve.tensor_copy(probs_t[:, j, 0], turn_bank[0][:, 0:TOKENS]).then_inc(turned0_ready, 1)

            def take_mixed(j):
                b, last = j % IMAGES, j >= IMAGES
                dve.wait_ge(mixed, j + 1)
                made = mix_bank[:, 0:TILES * VW].rearrange("p (t n) -> p t n", t=TILES)
                dve.reciprocal(inv_sum[:, j], made[:, :, C]).then_inc(inv_ready, 1)
                dve.wait_ge(inv_ready, j + 1)
                if last:
                    dve.wait_ge(y_const_ready, b + 1)
                else:
                    dve.wait_ge(xw2_ready, b + 1)
                for t in range(TILES):
                    dve.scalar_tensor_tensor(out=(result if last else pre)[:, b, t], in0=made[:, t, 0:C],
                                             scalar=inv_sum[:, j, t:t + 1],
                                             in1=(y_const if last else xw2)[:, b, t],
                                             op0=ALU.mult, op1=ALU.add).then_inc(mix_read, 1)
                if last:
                    return
                dve.wait_ge(mix_read, TILES * (j + 1))
                dve.tensor_scalar(y[:, b], pre[:, b], 0.0, None, ALU.max).then_inc(relu_ready, 1)
                dve.wait_ge(relu_ready, b + 1)
                for t in range(TILES):
                    dve.bn_stats(stats[:, b, t], y[:, b, t]).then_inc(stats_ready, 1)
                for t in range(TILES):
                    dve.wait_ge(stats_ready, TILES * b + t + 1)
                    dve.bn_aggr(mean_var[:, b, t], stats[:, b, t]).then_inc(mean_ready, 1)
                dve.wait_ge(mean_ready, TILES * (b + 1))
                dve.tensor_scalar(ln_var[:, b], mean_var[:, b, :, 1], LN_EPS, None, ALU.add).then_inc(ln_eps_added, 1)

            def normalise(b):
                dve.wait_ge(rstd_ready, b + 1)
                for t in range(TILES):
                    dve.tensor_scalar(normed[:, b, t], y[:, b, t], mean_var[:, b, t, 0:1], rstd[:, b, t:t + 1],
                                      ALU.subtract, ALU.mult).then_inc(normed_ready, 1)

            def take_h(b):
                dve.wait_ge(h_turned, b + 1)
                dve.tensor_scalar(h_t[:, b], q_bank[:, 0:TOKENS], col["ln_g"], col["ln_b"],
                                  ALU.mult, ALU.add).then_inc(h_ready, 1)

            def take_k(b):
                dve.wait_ge(qk_made, 2 * b + 2)
                dve.tensor_scalar(k_t[:, b], k_bank[:, 0:TOKENS], col["bk"], None, ALU.add).then_inc(k_ready, 1)

            steps = {"FG": take_f, "FOLD": folds, "N": maxima, "P": take_turned,
                     "O": take_mixed, "L": normalise, "H": take_h, "K": take_k}
            for step in DVE_ORDER:
                steps[step[:-1]](int(step[-1]))

        @block.tensor
        def _(pe):
            def make_fg(_):
                pe.wait_ge(first_in, 16)
                for n, weights in enumerate((wf2, wg2)):
                    for b in range(IMAGES):
                        mm = pe.matmul((q_bank, k_bank)[n][BLOCK * b:BLOCK * (b + 1), 0:TOKENS], weights,
                                       x_t[:, b * TOKENS:(b + 1) * TOKENS], start=True, stop=True)
                    mm.then_inc(fg_made, 1)

            def fold(n):
                if n == 0:
                    pe.wait_ge(fold0_in, 16)
                    pe.matmul(mix_bank[:, 0:C + 1], w["wo"][0:CV, :], wh_t_bh, start=True, stop=True)
                    pe.wait_ge(first_in, 16)
                    pe.matmul(mix_bank[:, C:C + 1], identity, col["bo"], start=False, stop=True,
                              skip_group_check=True).then_inc(wh_wo_made, 1)
                    pe.wait_ge(wh_wo_ready, 1)
                    pe.matmul(value_bank[:, 0:C + 1], w["wc_top"], wh_wo_t[:], start=True, stop=True).then_inc(w1_t_made, 1)
                    pe.wait_ge(w1_t_ready, 1)
                    pe.transpose(mix_bank[:, 0:C], w1_t[:], identity)
                    pe.wait_ge(w2_t_ready, 1)
                    pe.transpose(mix_bank[:, C:2 * C], w2_t[:], identity).then_inc(w1w2_made, 1)
                    pe.wait_ge(const0_col_ready, 1)
                    pe.matmul(turn_bank[0][:, 0:C], const0_col[:].to_broadcast([P, P]), identity,
                              start=True, stop=True).then_inc(const0_made, 1)
                else:
                    pe.wait_ge(fold1_in, 16)
                    pe.matmul(turn_bank[1][:, 0:C], w["wv_t"], w["wp"], start=True, stop=True).then_inc(wvp_made, 1)
                    pe.wait_ge(w1w2_ready, 1)
                    pe.matmul(mix_bank[:, 0:C], col["bv"].to_broadcast([P, P]), w["wp"], start=True, stop=False)
                    pe.matmul(mix_bank[:, 0:C], col["bp"].to_broadcast([P, P]), identity,
                              start=False, stop=True).then_inc(const1_made, 1)

            def make_scores(j):
                if j >= 2:
                    pe.wait_ge(probs_ready, TILES * (j - 1))
                if j < IMAGES:
                    if j == 0:
                        pe.wait_ge(f_ready, 1)
                        pe.wait_ge(g_ready, 1)
                    at = BLOCK * j
                    queries, keys = g_all[at:at + CK, :], f_all[at:at + CK, :]
                else:
                    b = j - IMAGES
                    pe.wait_ge(q_ready, b + 1)
                    pe.wait_ge(k_ready, b + 1)
                    queries, keys = q_t[:, b], k_t[:, b]
                for t in range(TILES):
                    pe.matmul(scores_of(j, t), queries[:, t * P:(t + 1) * P], keys, start=True,
                              stop=True).then_inc(scores_made, 1)

            def make_xv(j):
                if j == 0:
                    pe.wait_ge(w1w2_ready, 1)
                    pe.wait_ge(const0_col_ready, 1)
                else:
                    pe.wait_ge(values_ready, j)
                if j < IMAGES:
                    tokens, weights, span = x_t[:, j * TOKENS:(j + 1) * TOKENS], w1w2[:], 2 * C
                else:
                    if j == IMAGES:
                        pe.wait_ge(wvp_ready, 1)
                    pe.wait_ge(h_ready, j - IMAGES + 1)
                    tokens, weights, span = h_t[:, j - IMAGES], wvp[:], C
                for t in range(TILES):
                    mm = pe.matmul(value_bank[:, t * span:(t + 1) * span], tokens[:, t * P:(t + 1) * P], weights,
                                   start=True, stop=True)
                mm.then_inc(xv_made, 1)

            def turn(j):
                for t in range(TILES):
                    if j >= 1:
                        pe.wait_ge((turned0_ready, turned1_ready)[t], j)
                    elif t == 0:
                        pe.wait_ge(const0_ready, TILES)
                    else:
                        pe.wait_ge(wvp_ready, 1)
                    pe.wait_ge(probs_ready, TILES * j + t + 1)
                    for m in range(TILES):
                        mm = pe.transpose(turn_bank[t][:, m * P:(m + 1) * P], probs[:, j, t, m * P:(m + 1) * P], identity)
                    mm.then_inc(turned, 1)

            def mix(j):
                if j == 0:
                    pe.wait_ge(ones_set, 1)
                    pe.wait_ge(const1_ready, TILES)
                else:
                    pe.wait_ge(mix_read, TILES * j)
                pe.wait_ge(values_ready, j + 1)
                for t in range(TILES):
                    pe.wait_ge((turned0_ready, turned1_ready)[t], j + 1)
                    for m in range(TILES):
                        mm = pe.matmul(mix_bank[:, t * VW:t * VW + C + 1], probs_t[:, j, t, m * P:(m + 1) * P],
                                       values[:, j, m, 0, 0:C + 1], start=(m == 0), stop=(m == TILES - 1))
                mm.then_inc(mixed, 1)

            def turn_h(b):
                if b == 0:
                    pe.wait_ge(f_ready, 1)
                else:
                    pe.wait_ge(q_ready, b)
                for t in range(TILES):
                    pe.wait_ge(normed_ready, TILES * b + t + 1)
                    mm = pe.transpose(q_bank[:, t * P:(t + 1) * P], normed[:, b, t], identity)
                mm.then_inc(h_turned, 1)

            def make_qk(b):
                if b == 0:
                    pe.wait_ge(fold1_in, 16)
                pe.wait_ge(h_ready, b + 1)
                if b == 0:
                    pe.wait_ge(g_ready, 1)
                else:
                    pe.wait_ge(k_ready, b)
                for out_bank, name in ((q_bank, "wq"), (k_bank, "wk")):
                    pe.matmul(out_bank[:, 0:TOKENS], w[name], h_t[:, b], start=True,
                              stop=True).then_inc(qk_made, 1)

            steps = {"FG": make_fg, "FOLD": fold, "S": make_scores, "X": make_xv, "V": make_xv, "T": turn,
                     "M": mix, "H": turn_h, "Q": make_qk}
            for step in PE_ORDER:
                steps[step[:-1]](int(step[-1]))


OUT_SHAPE = (IMAGES, 16, 16, C)


def kernel(**inputs):
    import numpy as np
    import concourse.bacc as bacc
    from concourse.bass_utils import run_bass_kernel_spmd

    given = {n.removeprefix("L0_conv_").removeprefix("L1_conv_"): np.asarray(a) for n, a in inputs.items()}

    def padded(a, columns):
        out = np.zeros((P, columns), np.float32)
        out[:a.shape[0], :a.shape[1]] = a
        return out

    def column(name):
        a = given[name].reshape(-1)
        if name in ("bf", "bg"):
            a = np.tile(a, P // CK)
        if name == "gamma":
            a = np.tile(a, P)
        return padded(a[:, None], 1)

    wc = given["wc"]
    blocks = {
        "wo": given["wo"], "wh_t": given["wh"].T, "bh": given["bh"][:, None], "wc_top": wc[:C], "wc_top_t": wc[:C].T,
        "wc_bottom_t": wc[C:].T, "identity": np.eye(C),
        "wv_t": given["Wv"].T, "wp": given["Wp"], "wq": given["Wq"], "wk": given["Wk"],
    }
    arrays = {
        "first": np.concatenate([given["x"].reshape(IMAGES * TOKENS, C).T]
                                + [given[n] for n in ("wf", "wf", "wg", "wg")]
                                + [column(n) for n in COL_NAMES], axis=1),
        "fold0": np.concatenate([padded(blocks[n], blocks[n].shape[1]) for n in FOLD0], axis=1),
        "fold1": np.concatenate([blocks[n] for n in FOLD1], axis=1),
    }
    arrays = {n: np.ascontiguousarray(a) for n, a in arrays.items()}
    nc = bacc.Bacc("TRN2", target_bir_lowering=False, num_devices=1)
    args = [nc.dram_tensor(n, a.shape, F32, kind="ExternalInput").ap() for n, a in arrays.items()]
    out = nc.dram_tensor("out", (IMAGES, TOKENS, C), F32, kind="ExternalOutput").ap()
    attention_blocks(nc, *args, out)
    got = run_bass_kernel_spmd(nc, [arrays], core_ids=[0])
    return got.results[0]["out"].reshape(OUT_SHAPE)
```

```python
from contextlib import ExitStack

import concourse.bass as bass
from concourse import mybir

F32 = mybir.dt.float32
F32R = mybir.dt.float32r
BF16 = mybir.dt.bfloat16
ALU = mybir.AluOpType
ACT = mybir.ActivationFunctionType
AX_X = mybir.AxisListType.X

P = 128
IMAGES = 4
TOKENS = 256
TILES = TOKENS // P
C = 128
CK = C // 8
CV = C // 2
BLOCK = 32
VW = C + 2
ATTENTIONS = 2 * IMAGES
BN_EPS = 1e-3
LN_EPS = 1e-3
SCORE_SCALE = float(C) ** -0.5

X0, FG_W, COLS = 0, IMAGES * TOKENS, IMAGES * TOKENS + 2 * BLOCK
COL_NAMES = ["bf", "bg", "gamma", "bo", "ln_g", "ln_b", "bq", "bk", "bv", "bp",
             "bn_var", "bn_scale", "bc", "bn_mean", "bn_bias", "low_half"]
FIRST_W = COLS + len(COL_NAMES)
FOLD0 = ["wo", "wh_t", "bh", "wc_top", "wc_top_t", "wc_bottom_t", "identity"]
FOLD0_W = (len(FOLD0) - 1) * C + 1
FOLD1 = ["wv_t", "wp", "wq_t", "wk_t"]


PE_ORDER = """W0 W1 W1 W1 W1 W1 W1 W1 F0 A0 W1 W1 B0 W1 W1 K0 C0 D0 S0 S1 J0 X0 G0 T0 S2 X1 M0 T1 X2 S3 M1 X3 T2
        H0 M2 Q0 T3 S4 H1 V4 M3 Q1 V5 T4 H2 S5 Q2 M4 H3 S6 Q3 V6 T5 S7 M5 V7 T6 M6 T7 M7""".split()
POOL_ORDER = """X0 C0 X2 C1 R0 C2 Y0 R1 C3 R2 R3 Y1 Y2 Y3""".split()
ACT_ORDER = """A0 G0 C0 W0 E0 M0 P00 P01 E1 V1 P10 P11 Y0 V2 E2 E3 V3 P20 Y1 P21 H0 Q0 Y2 P30 P31 H1 V4 E4 Q1 P41
        H2 P40 V5 Q2 H3 E5 Q3 P50 P51 V6 E6 V7 P60 P61 E7 P70 P71""".split()
DVE_ORDER = """A0 X1 F0 B0 C0 G0 D0 N0 I0 J0 V0 N1 N2 X3 R0 O0 S00 S01 N3 M0 R1 E0 O1 L0 S10 S11 M1 E1 R2 O2 L1 S20
        S21 M2 E2 N4 L2 T0 R3 O3 Y3 S30 S31 M3 E3 L3 N5 R4 T1 O4 N6 T2 N7 R5 O5 T3 R6 O6 R7 O7""".split()


def attention_blocks(nc, first, fold0, fold1, out):
    with ExitStack() as ctx:
        def sb(name, shape, dtype=F32):
            return ctx.enter_context(nc.sbuf_tensor(name, shape, dtype))

        def bank(name):
            return ctx.enter_context(nc.psum_tensor(name, [P, 512], F32))

        def sem(name):
            return ctx.enter_context(nc.semaphore(name))

        first_sb = sb("first_sb", [P, FIRST_W])
        fold0_sb = sb("fold0_sb", [P, FOLD0_W])
        fold1_sb = sb("fold1_sb", [P, len(FOLD1) * C])
        minus_half = sb("minus_half", [P, TILES])
        var_eps = sb("var_eps", [P, 1])
        power = sb("power", [P, 1])
        bn_a = sb("bn_a", [P, 1])
        gamma_a = sb("gamma_a", [P, 1])
        centre = sb("centre", [P, 1])
        shift = sb("shift", [P, 1])
        both_t = sb("both_t", [P, C])
        wh_wo_t = sb("wh_wo_t", [P, C + 1])
        w1_t = sb("w1_t", [P, C])
        w2_t = sb("w2_t", [P, C])
        const0_col = sb("const0_col", [P, 1])
        w1w2_high = sb("w1w2_high", [P, 2 * C], F32R)
        w1w2_low = sb("w1w2_low", [P, 2 * C], F32R)
        x_high = sb("x_high", [P, IMAGES, TOKENS], F32R)
        x_low = sb("x_low", [P, IMAGES, TOKENS], F32R)
        zeros = sb("zeros", [P, P], BF16)
        const0 = sb("const0", [P, 1, C])
        wvp = sb("wvp", [P, C + 1])
        const1 = sb("const1", [P, 1, C])
        f_all = sb("f_all", [P, TOKENS])
        g_all = sb("g_all", [P, TOKENS])
        f_high = sb("f_high", [P, TOKENS], F32R)
        f_parts = sb("f_parts", [P, TOKENS], F32R)
        g_high = sb("g_high", [P, TOKENS], F32R)
        g_low = sb("g_low", [P, TOKENS], F32R)
        values = sb("values", [P, ATTENTIONS, TILES, 2, VW])
        xw2 = sb("xw2", [P, IMAGES, TILES, C])
        neg_max = sb("neg_max", [P, ATTENTIONS, TILES])
        probs = sb("probs", [P, ATTENTIONS, TILES, TOKENS])
        probs_t = sb("probs_t", [P, ATTENTIONS, TILES, TOKENS])
        inv_sum = sb("inv_sum", [P, ATTENTIONS, TILES])
        pre = sb("pre", [P, IMAGES, TILES, C])
        y = sb("y", [P, IMAGES, TILES, C])
        y_const = sb("y_const", [P, IMAGES, TILES, C])
        stats = sb("stats", [P, IMAGES, TILES, 6])
        mean_var = sb("mean_var", [P, IMAGES, TILES, 2])
        ln_var = sb("ln_var", [P, IMAGES, TILES])
        rstd = sb("rstd", [P, IMAGES, TILES])
        normed = sb("normed", [P, IMAGES, TILES, C])
        h_t = sb("h_t", [P, IMAGES, TOKENS])
        q_t = sb("q_t", [P, IMAGES, TOKENS])
        wqk = sb("wqk", [P, C])
        bq_wk = sb("bq_wk", [P, 1])
        bq_bk = sb("bq_bk", [P, 1])
        true_neg_max = sb("true_neg_max", [P, IMAGES, TILES])
        exp_bias = sb("exp_bias", [P, IMAGES, TILES])
        result = sb("result", [P, IMAGES, TILES, C])

        score_bank = [bank(f"score_bank{i}") for i in range(2)]
        turn_bank = [bank(f"turn_bank{t}") for t in range(TILES)]
        mix_banks = [bank(f"mix_bank{i}") for i in range(2)]
        mix_bank, g_bank = mix_banks
        value_bank = bank("value_bank")
        q_bank = bank("q_bank")

        x_t = first_sb[:, X0:X0 + IMAGES * TOKENS]
        wf2 = first_sb[:, FG_W:FG_W + BLOCK]
        wg2 = first_sb[:, FG_W + BLOCK:FG_W + 2 * BLOCK]
        col = {n: first_sb[:, COLS + i:COLS + i + 1] for i, n in enumerate(COL_NAMES)}
        w, at = {}, 0
        for n in FOLD0:
            w[n] = fold0_sb[:, at:at + (1 if n == "bh" else C)]
            at += 1 if n == "bh" else C
        for i, n in enumerate(FOLD1):
            w[n] = fold1_sb[:, i * C:(i + 1) * C]
        wh_t_bh = fold0_sb[0:CV, C:2 * C + 1]
        identity = w["identity"]

        first_in, fold0_in, fold1_in = (sem(n) for n in ("first_in", "fold0_in", "fold1_in"))
        half_set = sem("half_set")
        ones_set = sem("ones_set")
        fg_made = sem("fg_made")
        zeros_set = sem("zeros_set")
        f_ready = sem("f_ready")
        f_high_ready = sem("f_high_ready")
        f_parts_ready = sem("f_parts_ready")
        g_ready = sem("g_ready")
        g_high_ready = sem("g_high_ready")
        g_low_ready = sem("g_low_ready")
        x_high_ready = [sem(f"x_high_ready{b}") for b in range(IMAGES)]
        x_low_ready = [sem(f"x_low_ready{b}") for b in range(IMAGES)]
        eps_added = sem("eps_added")
        powered = sem("powered")
        a_ready = sem("a_ready")
        gamma_a_ready = sem("gamma_a_ready")
        centred = sem("centred")
        shift_ready = sem("shift_ready")
        both_added = sem("both_added")
        wh_wo_made = sem("wh_wo_made")
        wh_wo_ready = sem("wh_wo_ready")
        w1_t_made = sem("w1_t_made")
        w1_t_ready = sem("w1_t_ready")
        w2_t_ready = sem("w2_t_ready")
        const0_col_ready = sem("const0_col_ready")
        w1w2_made = sem("w1w2_made")
        w1w2_high_ready = sem("w1w2_high_ready")
        w1w2_low_ready = sem("w1w2_low_ready")
        const0_made = sem("const0_made")
        const0_ready = sem("const0_ready")
        wvp_made = sem("wvp_made")
        wvp_ready = sem("wvp_ready")
        const1_made = sem("const1_made")
        const1_ready = sem("const1_ready")
        scores_made = sem("scores_made")
        max_ready = sem("max_ready")
        probs_ready = sem("probs_ready")
        turned = sem("turned")
        turned_ready = [sem(f"turned_ready{t}") for t in range(TILES)]
        xv_made = sem("xv_made")
        values_ready = sem("values_ready")
        xw2_ready = sem("xw2_ready")
        mixed = sem("mixed")
        inv_ready = sem("inv_ready")
        mix_read = sem("mix_read")
        relu_ready = sem("relu_ready")
        y_const_ready = sem("y_const_ready")
        stats_ready = sem("stats_ready")
        mean_ready = sem("mean_ready")
        ln_eps_added = sem("ln_eps_added")
        rstd_ready = sem("rstd_ready")
        normed_ready = sem("normed_ready")
        h_turned = sem("h_turned")
        h_ready = sem("h_ready")
        q_made = sem("q_made")
        q_ready = sem("q_ready")
        wqk_made = sem("wqk_made")
        wq_bk_ready = sem("wq_bk_ready")
        wqk_ready = sem("wqk_ready")
        bq_folds_ready = sem("bq_folds_ready")
        true_max_ready = sem("true_max_ready")
        exp_bias_ready = sem("exp_bias_ready")
        stored = sem("stored")

        block = ctx.enter_context(nc.Block())

        @block.sync
        def _(sp):
            sp.dma_start(first_sb[:], first).then_inc(first_in, 16)
            sp.dma_start(fold1_sb[:], fold1).then_inc(fold1_in, 16)
            for b in range(IMAGES):
                sp.wait_ge(mix_read, TILES * (IMAGES + b + 1))
                sp.dma_start(out[b].rearrange("(t p) c -> p t c", p=P), result[:, b]).then_inc(stored, 16)
            sp.wait_ge(stored, 16 * IMAGES)

        def x_of(b):
            return x_t[:, b * TOKENS:(b + 1) * TOKENS]

        def scores_of(j, t):
            return score_bank[j % 2][:, t * TOKENS:(t + 1) * TOKENS]

        @block.gpsimd
        def _(pool):
            pool.memset(minus_half[:], -0.5).then_inc(half_set, 1)
            pool.memset(values[:, :, :, 0, C:VW], 1.0).then_inc(ones_set, 1)
            pool.wait_ge(half_set, 1)
            pool.wait_ge(eps_added, 1)
            pool.tensor_tensor(out=power[:], in0=var_eps[:], in1=minus_half[:, 0:1], op=ALU.pow).then_inc(powered, 1)

            def split_x(b):
                pool.wait_ge(first_in, 16)
                pool.tensor_copy(x_high[:, b], x_of(b)).then_inc(x_high_ready[b], 1)
                pool.wait_ge(x_high_ready[b], 1)
                pool.tensor_tensor(out=x_low[:, b], in0=x_of(b), in1=x_high[:, b].bitcast(F32),
                                   op=ALU.subtract).then_inc(x_low_ready[b], 1)

            def add_const0(b):
                pool.wait_ge(const0_ready, 1)
                pool.wait_ge(values_ready, b + 1)
                pool.tensor_tensor(out=xw2[:, b], in0=values[:, b, :, 1, 0:C], in1=const0[:].to_broadcast([P, TILES, C]),
                                   op=ALU.add).then_inc(xw2_ready, 1)

            def root(b):
                pool.wait_ge(ln_eps_added, b + 1)
                pool.tensor_tensor(out=rstd[:, b], in0=ln_var[:, b], in1=minus_half[:],
                                   op=ALU.pow).then_inc(rstd_ready, 1)

            def add_const1(b):
                pool.wait_ge(const1_ready, 1)
                pool.wait_ge(relu_ready, b + 1)
                pool.tensor_tensor(out=y_const[:, b], in0=y[:, b], in1=const1[:].to_broadcast([P, TILES, C]),
                                   op=ALU.add).then_inc(y_const_ready, 1)

            steps = {"X": split_x, "C": add_const0, "R": root, "Y": add_const1}
            for step in POOL_ORDER:
                steps[step[0]](int(step[1]))

        @block.scalar
        def _(act):
            act.dma_start(fold0_sb[:], fold0).then_inc(fold0_in, 16)

            def take_g(_):
                act.wait_ge(first_in, 16)
                act.wait_ge(fg_made, 2)
                act.activation(g_high[:], g_bank[:, 0:TOKENS], ACT.Identity,
                               bias=col["bg"]).then_inc(g_high_ready, 1)
                act.activation(g_all[:], g_bank[:, 0:TOKENS], ACT.Identity,
                               bias=col["bg"]).then_inc(g_ready, 1)

            def take_wh_wo(_):
                act.wait_ge(wh_wo_made, 1)
                act.activation(wh_wo_t[:], mix_bank[:, 0:C + 1], ACT.Copy).then_inc(wh_wo_ready, 1)

            def take_w1w2(_):
                act.wait_ge(w1w2_made, 1)
                act.activation(w1w2_high[:], mix_bank[:, 0:2 * C], ACT.Copy).then_inc(w1w2_high_ready, 1)

            def take_wvp(_):
                act.wait_ge(wvp_made, 1)
                act.activation(wvp[:, 0:C], turn_bank[1][:, 0:C], ACT.Copy).then_inc(wvp_ready, 1)

            def take_wqk(_):
                act.wait_ge(wqk_made, 1)
                act.activation(wqk[:], g_bank[:, 0:C], ACT.Copy, scale=SCORE_SCALE).then_inc(wqk_ready, 1)
                act.activation(wvp[:, C:C + 1], g_bank[:, C:C + 1], ACT.Copy, scale=SCORE_SCALE).then_inc(wq_bk_ready, 1)
                act.activation(bq_wk[:], g_bank[:, C + 1:C + 2], ACT.Copy, scale=SCORE_SCALE).then_inc(bq_folds_ready, 1)
                act.activation(bq_bk[:], g_bank[:, C + 2:C + 3], ACT.Copy, scale=SCORE_SCALE).then_inc(bq_folds_ready, 1)

            def exponentials(j):
                act.wait_ge(scores_made, TILES * (j + 1))
                if j < IMAGES:
                    act.wait_ge(max_ready, j + 1)
                    bias = neg_max[:, j]
                else:
                    act.wait_ge(exp_bias_ready, j - IMAGES + 1)
                    bias = exp_bias[:, j - IMAGES]
                for t in range(TILES):
                    act.activation(probs[:, j, t], scores_of(j, t), ACT.Exp, bias=bias[:, t:t + 1]).then_inc(probs_ready, 1)

            def take_values(j):
                act.wait_ge(xv_made, j + 1)
                act.wait_ge(ones_set, 1)
                if j < IMAGES:
                    made = value_bank[:].rearrange("p (t k n) -> p t k n", t=TILES, k=2)
                    taken = values[:, j, :, :, 0:C]
                else:
                    made = value_bank[:, 0:TILES * (C + 1)].rearrange("p (t n) -> p t n", t=TILES)
                    taken = values[:, j, :, 0, 0:C + 1]
                act.activation(taken, made, ACT.Copy).then_inc(values_ready, 1)

            def take_turned(j, t):
                act.wait_ge(turned, TILES * j + t + 1)
                act.activation(probs_t[:, j, t], turn_bank[t][:, 0:TOKENS], ACT.Copy).then_inc(turned_ready[t], 1)

            def take_h(b):
                act.wait_ge(h_turned, b + 1)
                act.activation(h_t[:, b], q_bank[:, 0:TOKENS], ACT.Identity, bias=col["ln_b"],
                               scale=col["ln_g"]).then_inc(h_ready, 1)

            def relu(b):
                act.wait_ge(mix_read, TILES * (b + 1))
                act.activation(y[:, b], pre[:, b], ACT.Relu).then_inc(relu_ready, 1)

            def take_q(b):
                act.wait_ge(q_made, b + 1)
                act.wait_ge(bq_folds_ready, 2)
                act.activation(q_t[:, b], q_bank[:, 0:TOKENS], ACT.Identity, bias=bq_wk[:]).then_inc(q_ready, 1)

            steps = {"G": take_g, "A": take_wh_wo, "C": take_w1w2, "W": take_wvp, "M": take_wqk, "E": exponentials, "V": take_values,
                     "P": take_turned, "H": take_h, "Q": take_q, "Y": relu}
            for step in ACT_ORDER:
                steps[step[0]](*map(int, step[1:]))

        @block.vector
        def _(dve):
            dve.memset(zeros[:], 0.0).then_inc(zeros_set, 1)

            def take_f(_):
                dve.wait_ge(first_in, 16)
                dve.wait_ge(fg_made, 1)
                dve.tensor_scalar(f_all[:], q_bank[:, 0:TOKENS], col["bf"], None, ALU.add).then_inc(f_ready, 1)
                dve.wait_ge(f_ready, 1)
                dve.tensor_copy(f_high[:], f_all[:]).then_inc(f_high_ready, 1)
                dve.wait_ge(f_high_ready, 1)
                dve.scalar_tensor_tensor(out=f_parts[:], in0=f_high[:].bitcast(F32), scalar=col["low_half"], in1=f_all[:],
                                         op0=ALU.mult, op1=ALU.add).then_inc(f_parts_ready, 1)

            def split_g(_):
                dve.wait_ge(g_high_ready, 1)
                dve.wait_ge(g_ready, 1)
                dve.tensor_tensor(out=g_low[:], in0=g_all[:], in1=g_high[:].bitcast(F32),
                                  op=ALU.subtract).then_inc(g_low_ready, 1)

            def split_x(b):
                dve.wait_ge(first_in, 16)
                dve.tensor_copy(x_high[:, b], x_of(b)).then_inc(x_high_ready[b], 1)
                dve.wait_ge(x_high_ready[b], 1)
                dve.tensor_tensor(out=x_low[:, b], in0=x_of(b), in1=x_high[:, b].bitcast(F32),
                                  op=ALU.subtract).then_inc(x_low_ready[b], 1)

            def fold_norm(_):
                dve.wait_ge(first_in, 16)
                dve.tensor_scalar(var_eps[:], col["bn_var"], BN_EPS, None, ALU.add).then_inc(eps_added, 1)
                dve.tensor_tensor(out=centre[:], in0=col["bc"], in1=col["bn_mean"], op=ALU.subtract).then_inc(centred, 1)

            def fold_a(_):
                dve.wait_ge(fold0_in, 16)
                dve.tensor_tensor(out=both_t[:], in0=w["wc_top_t"], in1=w["wc_bottom_t"],
                                  op=ALU.add).then_inc(both_added, 1)
                dve.wait_ge(powered, 1)
                dve.tensor_tensor(out=bn_a[:], in0=power[:], in1=col["bn_scale"], op=ALU.mult).then_inc(a_ready, 1)
                dve.wait_ge(a_ready, 1)
                dve.tensor_tensor(out=gamma_a[:], in0=bn_a[:], in1=col["gamma"], op=ALU.mult).then_inc(gamma_a_ready, 1)
                dve.wait_ge(centred, 1)
                dve.scalar_tensor_tensor(out=shift[:], in0=centre[:], scalar=bn_a[:], in1=col["bn_bias"],
                                         op0=ALU.mult, op1=ALU.add).then_inc(shift_ready, 1)
                dve.wait_ge(both_added, 1)
                dve.tensor_scalar(w2_t[:], both_t[:], bn_a[:], None, ALU.mult).then_inc(w2_t_ready, 1)

            def fold_w1(_):
                dve.wait_ge(gamma_a_ready, 1)
                dve.wait_ge(w1_t_made, 1)
                dve.tensor_scalar(w1_t[:], value_bank[:, 0:C], gamma_a[:], None, ALU.mult).then_inc(w1_t_ready, 1)
                dve.wait_ge(shift_ready, 1)
                dve.scalar_tensor_tensor(out=const0_col[:], in0=value_bank[:, C:C + 1], scalar=gamma_a[:],
                                         in1=shift[:], op0=ALU.mult, op1=ALU.add).then_inc(const0_col_ready, 1)

            def split_w1w2(_):
                dve.wait_ge(w1w2_high_ready, 1)
                dve.tensor_tensor(out=w1w2_low[:], in0=mix_bank[:, 0:2 * C], in1=w1w2_high[:].bitcast(F32),
                                  op=ALU.subtract).then_inc(w1w2_low_ready, 1)

            def take_const0(_):
                dve.wait_ge(const0_made, 1)
                dve.tensor_copy(const0[:, 0], turn_bank[0][:, 0:C]).then_inc(const0_ready, 1)

            def take_const1(_):
                dve.wait_ge(const1_made, 1)
                dve.tensor_copy(const1[:, 0], mix_bank[:, 0:C]).then_inc(const1_ready, 1)

            def maxima(j):
                dve.wait_ge(scores_made, TILES * (j + 1))
                dve.tensor_reduce(neg_max[:, j], score_bank[j % 2][:].rearrange("p (t m) -> p t m", t=TILES),
                                  AX_X, ALU.max, negate=True).then_inc(max_ready, 1)

            def shift_maxima(b):
                j = IMAGES + b
                dve.wait_ge(max_ready, j + 1)
                dve.wait_ge(values_ready, j + 1)
                dve.wait_ge(bq_folds_ready, 2)
                h_wq_bk = values[:, j, :, 0, C]
                dve.scalar_tensor_tensor(out=true_neg_max[:, b], in0=neg_max[:, j], scalar=bq_bk[:], in1=h_wq_bk,
                                         op0=ALU.subtract, op1=ALU.subtract).then_inc(true_max_ready, 1)
                dve.wait_ge(true_max_ready, b + 1)
                dve.scalar_tensor_tensor(out=exp_bias[:, b], in0=true_neg_max[:, b], scalar=bq_bk[:], in1=h_wq_bk,
                                         op0=ALU.add, op1=ALU.add).then_inc(exp_bias_ready, 1)

            def take_turned(j, t):
                dve.wait_ge(turned, TILES * j + t + 1)
                dve.tensor_copy(probs_t[:, j, t], turn_bank[t][:, 0:TOKENS]).then_inc(turned_ready[t], 1)

            def take_values(j):
                dve.wait_ge(xv_made, j + 1)
                dve.wait_ge(ones_set, 1)
                if j < IMAGES:
                    made = value_bank[:].rearrange("p (t k n) -> p t k n", t=TILES, k=2)
                    taken = values[:, j, :, :, 0:C]
                else:
                    made = value_bank[:, 0:TILES * (C + 1)].rearrange("p (t n) -> p t n", t=TILES)
                    taken = values[:, j, :, 0, 0:C + 1]
                dve.tensor_copy(taken, made).then_inc(values_ready, 1)

            def take_q(b):
                dve.wait_ge(q_made, b + 1)
                dve.wait_ge(bq_folds_ready, 2)
                dve.tensor_scalar(q_t[:, b], q_bank[:, 0:TOKENS], bq_wk[:], None, ALU.add).then_inc(q_ready, 1)

            def mixed_of(j):
                return mix_banks[j % 2][:, 0:TILES * VW].rearrange("p (t n) -> p t n", t=TILES)

            def invert(j):
                dve.wait_ge(mixed, j + 1)
                dve.reciprocal(inv_sum[:, j], mixed_of(j)[:, :, C + 1]).then_inc(inv_ready, 1)

            def take_mixed(j):
                b, last = j % IMAGES, j >= IMAGES
                dve.wait_ge(inv_ready, j + 1)
                if last:
                    dve.wait_ge(y_const_ready, b + 1)
                else:
                    dve.wait_ge(xw2_ready, b + 1)
                for t in range(TILES):
                    dve.scalar_tensor_tensor(out=(result if last else pre)[:, b, t], in0=mixed_of(j)[:, t, 0:C],
                                             scalar=inv_sum[:, j, t:t + 1],
                                             in1=(y_const if last else xw2)[:, b, t],
                                             op0=ALU.mult, op1=ALU.add).then_inc(mix_read, 1)

            def relu(b):
                dve.wait_ge(mix_read, TILES * (b + 1))
                dve.tensor_scalar(y[:, b], pre[:, b], 0.0, None, ALU.max).then_inc(relu_ready, 1)

            def statistics(b, t):
                dve.wait_ge(relu_ready, b + 1)
                dve.bn_stats(stats[:, b, t], y[:, b, t]).then_inc(stats_ready, 1)

            def aggregate(b):
                for t in range(TILES):
                    dve.wait_ge(stats_ready, TILES * b + t + 1)
                    dve.bn_aggr(mean_var[:, b, t], stats[:, b, t]).then_inc(mean_ready, 1)

            def add_ln_eps(b):
                dve.wait_ge(mean_ready, TILES * (b + 1))
                dve.tensor_scalar(ln_var[:, b], mean_var[:, b, :, 1], LN_EPS, None, ALU.add).then_inc(ln_eps_added, 1)

            def normalise(b):
                dve.wait_ge(rstd_ready, b + 1)
                for t in range(TILES):
                    dve.tensor_scalar(normed[:, b, t], y[:, b, t], mean_var[:, b, t, 0:1], rstd[:, b, t:t + 1],
                                      ALU.subtract, ALU.mult).then_inc(normed_ready, 1)

            def take_h(b):
                dve.wait_ge(h_turned, b + 1)
                dve.tensor_scalar(h_t[:, b], q_bank[:, 0:TOKENS], col["ln_g"], col["ln_b"],
                                  ALU.mult, ALU.add).then_inc(h_ready, 1)

            steps = {"A": fold_norm, "F": take_f, "G": split_g, "X": split_x, "B": fold_a, "C": fold_w1, "D": split_w1w2,
                     "I": take_const0, "J": take_const1, "N": maxima, "T": shift_maxima, "P": take_turned, "V": take_values,
                     "R": invert, "O": take_mixed, "Y": relu, "S": statistics, "M": aggregate, "E": add_ln_eps,
                     "L": normalise, "H": take_h, "Q": take_q}
            for step in DVE_ORDER:
                steps[step[0]](*map(int, step[1:]))

        @block.tensor
        def _(pe):
            def warm_up(n):
                if n == 0:
                    pe.wait_ge(zeros_set, 1)
                pe.matmul(score_bank[1][:].rearrange("p (k n) -> p k n", n=P), zeros[:],
                          zeros[:].rearrange("p (k n) -> p k n", k=1).to_broadcast([P, 4, P]), start=True, stop=True)

            def make_fg(_):
                pe.wait_ge(first_in, 16)
                for n, weights in enumerate((wf2, wg2)):
                    for b in range(IMAGES):
                        mm = pe.matmul((q_bank, g_bank)[n][BLOCK * b:BLOCK * (b + 1), 0:TOKENS], weights,
                                       x_t[:, b * TOKENS:(b + 1) * TOKENS], start=True, stop=True)
                    mm.then_inc(fg_made, 1)

            def fold_wh_wo(_):
                pe.wait_ge(fold0_in, 16)
                pe.matmul(mix_bank[:, 0:C + 1], w["wo"][0:CV, :], wh_t_bh, start=True, stop=True)
                pe.wait_ge(first_in, 16)
                pe.matmul(mix_bank[:, C:C + 1], identity, col["bo"], start=False, stop=True,
                          skip_group_check=True).then_inc(wh_wo_made, 1)

            def fold_w1(_):
                pe.wait_ge(wh_wo_ready, 1)
                pe.matmul(value_bank[:, 0:C + 1], w["wc_top"], wh_wo_t[:], start=True, stop=True).then_inc(w1_t_made, 1)

            def turn_w1w2(_):
                pe.wait_ge(w1_t_ready, 1)
                pe.transpose(mix_bank[:, 0:C], w1_t[:], identity)
                pe.wait_ge(w2_t_ready, 1)
                pe.transpose(mix_bank[:, C:2 * C], w2_t[:], identity).then_inc(w1w2_made, 1)

            def spread_const0(_):
                pe.wait_ge(const0_col_ready, 1)
                pe.matmul(turn_bank[0][:, 0:C], const0_col[:].to_broadcast([P, P]), identity,
                          start=True, stop=True).then_inc(const0_made, 1)

            def fold_wvp(_):
                pe.wait_ge(fold1_in, 16)
                pe.matmul(turn_bank[1][:, 0:C], w["wv_t"], w["wp"], start=True, stop=True).then_inc(wvp_made, 1)

            def fold_wqk(_):
                pe.wait_ge(fold1_in, 16)
                pe.wait_ge(g_high_ready, 1)
                pe.wait_ge(g_ready, 1)
                pe.matmul(g_bank[:, 0:C], w["wq_t"], w["wk_t"], start=True, stop=True)
                pe.matmul(g_bank[:, C:C + 1], w["wq_t"], col["bk"], start=True, stop=True)
                pe.matmul(g_bank[:, C + 1:C + 2], w["wk_t"], col["bq"], start=True, stop=True)
                pe.matmul(g_bank[:, C + 2:C + 3], col["bq"].to_broadcast([P, P]), col["bk"],
                          start=True, stop=True).then_inc(wqk_made, 1)

            def spread_const1(_):
                pe.wait_ge(w1w2_low_ready, 1)
                pe.matmul(mix_bank[:, 0:C], col["bv"].to_broadcast([P, P]), w["wp"], start=True, stop=False)
                pe.matmul(mix_bank[:, 0:C], col["bp"].to_broadcast([P, P]), identity,
                          start=False, stop=True).then_inc(const1_made, 1)

            def make_scores(j):
                if j >= 2:
                    pe.wait_ge(probs_ready, TILES * (j - 1))
                if j < IMAGES:
                    if j == 0:
                        pe.wait_ge(f_parts_ready, 1)
                        pe.wait_ge(g_high_ready, 1)
                        pe.wait_ge(g_low_ready, 1)
                    at = slice(BLOCK * j, BLOCK * (j + 1))
                    parts = [(g_high[at, :], f_parts[at, :]), (g_low[at, :], f_parts[at, :])]
                else:
                    b = j - IMAGES
                    pe.wait_ge(q_ready, b + 1)
                    parts = [(q_t[:, b], h_t[:, b])]
                for t in range(TILES):
                    for n, (queries, keys) in enumerate(parts):
                        mm = pe.matmul(scores_of(j, t), queries[:, t * P:(t + 1) * P], keys, start=(n == 0),
                                       stop=(n == len(parts) - 1))
                    mm.then_inc(scores_made, 1)

            def make_xv(j):
                if j == 0:
                    pe.wait_ge(w1w2_high_ready, 1)
                    pe.wait_ge(w1w2_low_ready, 1)
                    pe.wait_ge(const0_col_ready, 1)
                else:
                    pe.wait_ge(values_ready, j)
                if j < IMAGES:
                    pe.wait_ge(x_high_ready[j], 1)
                    pe.wait_ge(x_low_ready[j], 1)
                    parts, span = [(x_high[:, j], w1w2_high[:]), (x_high[:, j], w1w2_low[:]), (x_low[:, j], w1w2_high[:])], 2 * C
                else:
                    if j == IMAGES:
                        pe.wait_ge(wvp_ready, 1)
                        pe.wait_ge(wq_bk_ready, 1)
                    pe.wait_ge(h_ready, j - IMAGES + 1)
                    parts, span = [(h_t[:, j - IMAGES], wvp[:])], C + 1
                for t in range(TILES):
                    for n, (tokens, weights) in enumerate(parts):
                        mm = pe.matmul(value_bank[:, t * span:(t + 1) * span], tokens[:, t * P:(t + 1) * P], weights,
                                       start=(n == 0), stop=(n == len(parts) - 1))
                mm.then_inc(xv_made, 1)

            def turn(j):
                for t in range(TILES):
                    if j >= 1:
                        pe.wait_ge(turned_ready[t], j)
                    elif t == 0:
                        pe.wait_ge(const0_ready, 1)
                    else:
                        pe.wait_ge(wvp_ready, 1)
                    pe.wait_ge(probs_ready, TILES * j + t + 1)
                    for m in range(TILES):
                        mm = pe.transpose(turn_bank[t][:, m * P:(m + 1) * P], probs[:, j, t, m * P:(m + 1) * P], identity)
                    mm.then_inc(turned, 1)

            def mix(j):
                if j == 0:
                    pe.wait_ge(ones_set, 1)
                    pe.wait_ge(const1_ready, 1)
                elif j == 1:
                    pe.wait_ge(bq_folds_ready, 2)
                else:
                    pe.wait_ge(mix_read, TILES * (j - 1))
                pe.wait_ge(values_ready, j + 1)
                for t in range(TILES):
                    pe.wait_ge(turned_ready[t], j + 1)
                    for m in range(TILES):
                        mm = pe.matmul(mix_banks[j % 2][:, t * VW:(t + 1) * VW], probs_t[:, j, t, m * P:(m + 1) * P],
                                       values[:, j, m, 0, :], start=(m == 0), stop=(m == TILES - 1))
                mm.then_inc(mixed, 1)

            def turn_h(b):
                if b == 0:
                    pe.wait_ge(f_ready, 1)
                else:
                    pe.wait_ge(q_ready, b)
                for t in range(TILES):
                    pe.wait_ge(normed_ready, TILES * b + t + 1)
                    mm = pe.transpose(q_bank[:, t * P:(t + 1) * P], normed[:, b, t], identity)
                mm.then_inc(h_turned, 1)

            def make_q(b):
                if b == 0:
                    pe.wait_ge(wqk_ready, 1)
                pe.wait_ge(h_ready, b + 1)
                pe.matmul(q_bank[:, 0:TOKENS], wqk[:], h_t[:, b], start=True, stop=True).then_inc(q_made, 1)

            steps = {"W": warm_up, "F": make_fg, "A": fold_wh_wo, "B": fold_w1, "C": turn_w1w2, "D": spread_const0,
                     "K": fold_wvp, "G": fold_wqk, "J": spread_const1, "S": make_scores, "X": make_xv, "V": make_xv, "T": turn,
                     "M": mix, "H": turn_h, "Q": make_q}
            for step in PE_ORDER:
                steps[step[0]](*map(int, step[1:]))


OUT_SHAPE = (IMAGES, 16, 16, C)


def kernel(**inputs):
    import numpy as np
    import concourse.bacc as bacc
    from concourse.bass_utils import run_bass_kernel_spmd

    given = {n.removeprefix("L0_conv_").removeprefix("L1_conv_"): np.asarray(a) for n, a in inputs.items()}

    def padded(a, columns):
        out = np.zeros((P, columns), np.float32)
        out[:a.shape[0], :a.shape[1]] = a
        return out

    def column(name):
        if name == "low_half":
            return -(np.arange(P) % BLOCK >= CK).astype(np.float32)[:, None]
        a = given[name].reshape(-1)
        if name in ("bf", "bg"):
            a = np.tile(a, P // CK)
        if name == "gamma":
            a = np.tile(a, P)
        return padded(a[:, None], 1)

    wc = given["wc"]
    blocks = {
        "wo": given["wo"], "wh_t": given["wh"].T, "bh": given["bh"][:, None], "wc_top": wc[:C], "wc_top_t": wc[:C].T,
        "wc_bottom_t": wc[C:].T, "identity": np.eye(C),
        "wv_t": given["Wv"].T, "wp": given["Wp"], "wq_t": given["Wq"].T, "wk_t": given["Wk"].T,
    }
    arrays = {
        "first": np.concatenate([given["x"].reshape(IMAGES * TOKENS, C).T]
                                + [given[n] for n in ("wf", "wf", "wg", "wg")]
                                + [column(n) for n in COL_NAMES], axis=1),
        "fold0": np.concatenate([padded(blocks[n], blocks[n].shape[1]) for n in FOLD0], axis=1),
        "fold1": np.concatenate([blocks[n] for n in FOLD1], axis=1),
    }
    arrays = {n: np.ascontiguousarray(a) for n, a in arrays.items()}
    nc = bacc.Bacc("TRN2", target_bir_lowering=False, num_devices=1)
    args = [nc.dram_tensor(n, a.shape, F32, kind="ExternalInput").ap() for n, a in arrays.items()]
    out = nc.dram_tensor("out", (IMAGES, TOKENS, C), F32, kind="ExternalOutput").ap()
    attention_blocks(nc, *args, out)
    got = run_bass_kernel_spmd(nc, [arrays], core_ids=[0])
    return got.results[0]["out"].reshape(OUT_SHAPE)
```

```python
from contextlib import ExitStack

import concourse.bass as bass
from concourse import mybir

F32 = mybir.dt.float32
F32R = mybir.dt.float32r
BF16 = mybir.dt.bfloat16
ALU = mybir.AluOpType
ACT = mybir.ActivationFunctionType
AX_X = mybir.AxisListType.X

P = 128
IMAGES = 4
TOKENS = 256
TILES = TOKENS // P
C = 128
CK = C // 8
CV = C // 2
BLOCK = 32
VW = C + 2
ATTENTIONS = 2 * IMAGES
BN_EPS = 1e-3
LN_EPS = 1e-3
SCORE_SCALE = float(C) ** -0.5

X0, FG_W = 0, IMAGES * TOKENS
COL_NAMES = ["bf", "bg", "gamma", "bo", "ln_g", "ln_b", "bq", "bv", "bp",
             "bn_var", "bn_scale", "bc", "bn_mean", "bn_bias", "low_half"]
FIRST_W = FG_W + 2 * BLOCK
FOLD0 = ["wo", "wh_t", "bh", "wc_top", "wc_top_t", "wc_bottom_t", "identity"]
COLS = (len(FOLD0) - 1) * C + 1
FOLD0_W = COLS + len(COL_NAMES)
FOLD1 = ["wv_t", "wp", "wq_t", "wk_t"]


PE_ORDER = """W0 W1 W1 W1 W1 W1 A0 W1 W1 W1 B0 F0 C0 G0 D0 K0 S0 S1 X0 J0 T0 S2 X1 M0 T1 S3 X2 M1 T2 X3 H0 M2 Q0
        V4 T3 S4 H1 M3 Q1 V5 T4 H2 S5 Q2 M4 H3 S6 V6 Q3 T5 V7 S7 T6 M5 M6 T7 M7""".split()
POOL_ORDER = """X0 X1 X2 X3 C0 C1 Y0 R0 C2 C3 R1 Y1 Y2 R2 Y3 R3""".split()
ACT_ORDER = """A0 G0 M0 W0 C0 E0 V0 P00 P01 E1 V1 E2 P11 P10 Y0 E3 V2 P20 P21 Y1 V3 Q0 Y2 V4 P31 P30 H1 E4 Q1 P40
        H2 P41 V5 Q2 H3 E5 V6 Q3 P51 E6 V7 P60 P61 E7 P70 P71""".split()
DVE_ORDER = """A0 B0 C0 F0 G0 D0 N0 I0 N1 J0 N2 R0 O0 N3 S00 S01 M0 E0 R1 O1 L0 S10 H0 S11 M1 R2 E1 O2 L1 S20 S21
        M2 N4 E2 T0 R3 O3 L2 Y3 S30 S31 M3 E3 L3 N5 R4 T1 N6 T2 P50 O4 K0 R5 O5 R6 O6 Z0""".split()


def attention_blocks(nc, first, fold0, fold1, out):
    with ExitStack() as ctx:
        def sb(name, shape, dtype=F32):
            return ctx.enter_context(nc.sbuf_tensor(name, shape, dtype))

        def bank(name):
            return ctx.enter_context(nc.psum_tensor(name, [P, 512], F32))

        def sem(name):
            return ctx.enter_context(nc.semaphore(name))

        first_sb = sb("first_sb", [P, FIRST_W])
        fold0_sb = sb("fold0_sb", [P, FOLD0_W])
        fold1_sb = sb("fold1_sb", [P, len(FOLD1) * C + 1])
        minus_half = sb("minus_half", [P, TILES])
        var_eps = sb("var_eps", [P, 1])
        power = sb("power", [P, 1])
        bn_a = sb("bn_a", [P, 1])
        gamma_a = sb("gamma_a", [P, 1])
        centre = sb("centre", [P, 1])
        shift = sb("shift", [P, 1])
        both_t = sb("both_t", [P, C])
        wh_wo_t = sb("wh_wo_t", [P, C + 1])
        w1_t = sb("w1_t", [P, C])
        w2_t = sb("w2_t", [P, C])
        const0_col = sb("const0_col", [P, 1])
        w1w2_high = sb("w1w2_high", [P, 2 * C], F32R)
        w1w2_low = sb("w1w2_low", [P, 2 * C], F32R)
        x_high = sb("x_high", [P, IMAGES, TOKENS], F32R)
        x_low = sb("x_low", [P, IMAGES, TOKENS], F32R)
        const0 = sb("const0", [P, 1, C])
        wvp = sb("wvp", [P, C + 1])
        const1 = sb("const1", [P, 1, C])
        f_all = sb("f_all", [P, TOKENS])
        g_all = sb("g_all", [P, TOKENS])
        f_high = sb("f_high", [P, TOKENS], F32R)
        f_parts = sb("f_parts", [P, TOKENS], F32R)
        g_high = sb("g_high", [P, TOKENS], F32R)
        g_low = sb("g_low", [P, TOKENS], F32R)
        values = sb("values", [P, ATTENTIONS, TILES, 2, VW])
        xw2 = sb("xw2", [P, IMAGES, TILES, C])
        neg_max = sb("neg_max", [P, ATTENTIONS, TILES])
        probs = sb("probs", [P, ATTENTIONS, TILES, TOKENS])
        probs_t = sb("probs_t", [P, ATTENTIONS, TILES, TOKENS])
        inv_sum = sb("inv_sum", [P, ATTENTIONS, TILES])
        pre = sb("pre", [P, IMAGES, TILES, C])
        y = sb("y", [P, IMAGES, TILES, C])
        y_const = sb("y_const", [P, IMAGES, TILES, C])
        stats = sb("stats", [P, IMAGES, TILES, 6])
        mean_var = sb("mean_var", [P, IMAGES, TILES, 2])
        ln_var = sb("ln_var", [P, IMAGES, TILES])
        rstd = sb("rstd", [P, IMAGES, TILES])
        normed = sb("normed", [P, IMAGES, TILES, C])
        h_t = sb("h_t", [P, IMAGES, TOKENS])
        q_t = sb("q_t", [P, IMAGES, TOKENS])
        wqk = sb("wqk", [P, C])
        bq_wk = sb("bq_wk", [P, 1])
        bq_bk = sb("bq_bk", [P, 1])
        true_neg_max = sb("true_neg_max", [P, IMAGES, TILES])
        exp_bias = sb("exp_bias", [P, IMAGES, TILES])
        result = sb("result", [P, IMAGES, TILES, C])

        score_bank = [bank(f"score_bank{i}") for i in range(2)]
        turn_bank = [bank(f"turn_bank{t}") for t in range(TILES)]
        mix_banks = [bank(f"fold_bank{i}") for i in range(2)]
        fold_bank, g_bank = mix_banks
        value_bank = bank("value_bank")
        q_bank = bank("q_bank")

        x_t = first_sb[:, X0:X0 + IMAGES * TOKENS]
        wf2 = first_sb[:, FG_W:FG_W + BLOCK]
        wg2 = first_sb[:, FG_W + BLOCK:FG_W + 2 * BLOCK]
        col = {n: fold0_sb[:, COLS + i:COLS + i + 1] for i, n in enumerate(COL_NAMES)}
        w, at = {}, 0
        for n in FOLD0:
            w[n] = fold0_sb[:, at:at + (1 if n == "bh" else C)]
            at += 1 if n == "bh" else C
        for i, n in enumerate(FOLD1):
            w[n] = fold1_sb[:, i * C:(i + 1) * C]
        wk_t_bk = fold1_sb[:, (len(FOLD1) - 1) * C:len(FOLD1) * C + 1]
        wh_t_bh = fold0_sb[0:CV, C:2 * C + 1]
        identity = w["identity"]

        first_in, fold0_in, fold1_in = (sem(n) for n in ("first_in", "fold0_in", "fold1_in"))
        minus_half_set = sem("minus_half_set")
        ones_set = sem("ones_set")
        fg_made = sem("fg_made")
        f_ready = sem("f_ready")
        f_high_ready = sem("f_high_ready")
        f_parts_ready = sem("f_parts_ready")
        g_ready = sem("g_ready")
        g_high_ready = sem("g_high_ready")
        g_low_ready = sem("g_low_ready")
        x_high_ready = [sem(f"x_high_ready{b}") for b in range(IMAGES)]
        x_low_ready = [sem(f"x_low_ready{b}") for b in range(IMAGES)]
        eps_added = sem("eps_added")
        powered = sem("powered")
        a_ready = sem("a_ready")
        gamma_a_ready = sem("gamma_a_ready")
        centred = sem("centred")
        shift_ready = sem("shift_ready")
        both_added = sem("both_added")
        wh_wo_made = sem("wh_wo_made")
        wh_wo_ready = sem("wh_wo_ready")
        w1_t_made = sem("w1_t_made")
        w1_t_ready = sem("w1_t_ready")
        w2_t_ready = sem("w2_t_ready")
        const0_col_ready = sem("const0_col_ready")
        w1w2_made = sem("w1w2_made")
        w1w2_high_ready = sem("w1w2_high_ready")
        w1w2_low_ready = sem("w1w2_low_ready")
        const0_made = sem("const0_made")
        const0_ready = sem("const0_ready")
        wvp_made = sem("wvp_made")
        wvp_ready = sem("wvp_ready")
        const1_made = sem("const1_made")
        const1_ready = sem("const1_ready")
        scores_made = sem("scores_made")
        max_ready = sem("max_ready")
        probs_ready = sem("probs_ready")
        turned = sem("turned")
        turned_ready = [sem(f"turned_ready{t}") for t in range(TILES)]
        xv_made = sem("xv_made")
        values_ready = sem("values_ready")
        xw2_ready = sem("xw2_ready")
        mixed = sem("mixed")
        inv_ready = sem("inv_ready")
        mix_read = sem("mix_read")
        relu_ready = sem("relu_ready")
        y_const_ready = sem("y_const_ready")
        stats_ready = sem("stats_ready")
        mean_ready = sem("mean_ready")
        ln_eps_added = sem("ln_eps_added")
        rstd_ready = sem("rstd_ready")
        normed_ready = sem("normed_ready")
        h_turned = sem("h_turned")
        h_ready = sem("h_ready")
        q_made = sem("q_made")
        q_ready = sem("q_ready")
        wqk_made = sem("wqk_made")
        wq_bk_ready = sem("wq_bk_ready")
        wqk_ready = sem("wqk_ready")
        bq_folds_ready = sem("bq_folds_ready")
        true_max_ready = sem("true_max_ready")
        exp_bias_ready = sem("exp_bias_ready")
        stored = sem("stored")

        block = ctx.enter_context(nc.Block())

        @block.sync
        def _(sp):
            sp.dma_start(fold0_sb[:], fold0).then_inc(fold0_in, 16)
            sp.dma_start(first_sb[:], first).then_inc(first_in, 16)
            sp.dma_start(fold1_sb[:], fold1).then_inc(fold1_in, 16)
            for b in range(IMAGES - 1):
                sp.wait_ge(mix_read, TILES * (IMAGES + b + 1))
                sp.dma_start(out[b].rearrange("(t p) c -> p t c", p=P), result[:, b]).then_inc(stored, 16)
            for t in range(TILES):
                sp.wait_ge(mix_read, TILES * (ATTENTIONS - 1) + t + 1)
                sp.dma_start(out[IMAGES - 1, t * P:(t + 1) * P, :], result[:, IMAGES - 1, t]).then_inc(stored, 16)
            sp.wait_ge(stored, 16 * (IMAGES - 1 + TILES))

        def x_of(b):
            return x_t[:, b * TOKENS:(b + 1) * TOKENS]

        def mixed_tile(j, t):
            if j < ATTENTIONS - 1:
                return mix_banks[j % 2][:, t * VW:(t + 1) * VW]
            return mix_banks[(j + t) % 2][:, 0:VW]

        def scores_of(j, t):
            if j == ATTENTIONS - 1 and t > 0:
                return q_bank[:, 0:TOKENS]
            return score_bank[j % 2][:, t * TOKENS:(t + 1) * TOKENS]

        @block.gpsimd
        def _(pool):
            pool.memset(minus_half[:], -0.5).then_inc(minus_half_set, 1)
            pool.memset(values[:, :, :, 0, C:VW], 1.0).then_inc(ones_set, 1)
            pool.wait_ge(minus_half_set, 1)
            pool.wait_ge(eps_added, 1)
            pool.tensor_tensor(out=power[:], in0=var_eps[:], in1=minus_half[:, 0:1], op=ALU.pow).then_inc(powered, 1)

            def split_x(b):
                pool.wait_ge(first_in, 16)
                pool.tensor_copy(x_high[:, b], x_of(b)).then_inc(x_high_ready[b], 1)
                pool.wait_ge(x_high_ready[b], 1)
                pool.tensor_tensor(out=x_low[:, b], in0=x_of(b), in1=x_high[:, b].bitcast(F32),
                                   op=ALU.subtract).then_inc(x_low_ready[b], 1)

            def add_const0(b):
                pool.wait_ge(const0_ready, 1)
                pool.wait_ge(values_ready, b + 1)
                pool.tensor_tensor(out=xw2[:, b], in0=values[:, b, :, 1, 0:C], in1=const0[:].to_broadcast([P, TILES, C]),
                                   op=ALU.add).then_inc(xw2_ready, 1)

            def root(b):
                pool.wait_ge(ln_eps_added, b + 1)
                pool.tensor_tensor(out=rstd[:, b], in0=ln_var[:, b], in1=minus_half[:],
                                   op=ALU.pow).then_inc(rstd_ready, 1)

            def add_const1(b):
                pool.wait_ge(const1_ready, 1)
                pool.wait_ge(relu_ready, b + 1)
                pool.tensor_tensor(out=y_const[:, b], in0=y[:, b], in1=const1[:].to_broadcast([P, TILES, C]),
                                   op=ALU.add).then_inc(y_const_ready, 1)

            steps = {"X": split_x, "C": add_const0, "R": root, "Y": add_const1}
            for step in POOL_ORDER:
                steps[step[0]](int(step[1]))

        @block.scalar
        def _(act):

            def take_g(_):
                act.wait_ge(fold0_in, 16)
                act.wait_ge(fg_made, 2)
                act.activation(g_high[:], g_bank[:, 0:TOKENS], ACT.Identity,
                               bias=col["bg"]).then_inc(g_high_ready, 1)
                act.activation(g_all[:], g_bank[:, 0:TOKENS], ACT.Identity,
                               bias=col["bg"]).then_inc(g_ready, 1)

            def take_wh_wo(_):
                act.wait_ge(wh_wo_made, 1)
                act.activation(wh_wo_t[:], fold_bank[:, 0:C + 1], ACT.Copy).then_inc(wh_wo_ready, 1)

            def take_w1w2(_):
                act.wait_ge(w1w2_made, 1)
                act.activation(w1w2_high[:], fold_bank[:, 0:2 * C], ACT.Copy).then_inc(w1w2_high_ready, 1)

            def take_wvp(_):
                act.wait_ge(wvp_made, 1)
                act.activation(wvp[:, 0:C], turn_bank[1][:, 0:C], ACT.Copy).then_inc(wvp_ready, 1)

            def take_wqk(_):
                act.wait_ge(wqk_made, 1)
                act.activation(wqk[:], score_bank[0][:, 0:C], ACT.Copy, scale=SCORE_SCALE).then_inc(wqk_ready, 1)
                act.activation(wvp[:, C:C + 1], score_bank[0][:, C:C + 1], ACT.Copy, scale=SCORE_SCALE).then_inc(wq_bk_ready, 1)
                act.activation(bq_wk[:], score_bank[0][:, C + 1:C + 2], ACT.Copy, scale=SCORE_SCALE).then_inc(bq_folds_ready, 1)
                act.activation(bq_bk[:], score_bank[0][:, C + 2:C + 3], ACT.Copy, scale=SCORE_SCALE).then_inc(bq_folds_ready, 1)

            def exponentials(j):
                for t in range(TILES):
                    if j == ATTENTIONS - 1:
                        act.wait_ge(exp_bias_ready, IMAGES + t)
                    elif t == 0:
                        if j < IMAGES:
                            act.wait_ge(max_ready, j + 1)
                        else:
                            act.wait_ge(exp_bias_ready, j - IMAGES + 1)
                    bias = neg_max[:, j] if j < IMAGES else exp_bias[:, j - IMAGES]
                    act.wait_ge(scores_made, TILES * j + t + 1)
                    act.activation(probs[:, j, t], scores_of(j, t), ACT.Exp, bias=bias[:, t:t + 1]).then_inc(probs_ready, 1)

            def take_values(j):
                act.wait_ge(xv_made, j + 1)
                act.wait_ge(ones_set, 1)
                if j < IMAGES:
                    made = value_bank[:].rearrange("p (t k n) -> p t k n", t=TILES, k=2)
                    taken = values[:, j, :, :, 0:C]
                else:
                    made = value_bank[:, 0:TILES * (C + 1)].rearrange("p (t n) -> p t n", t=TILES)
                    taken = values[:, j, :, 0, 0:C + 1]
                act.activation(taken, made, ACT.Copy).then_inc(values_ready, 1)

            def take_turned(j, t):
                act.wait_ge(turned, TILES * j + t + 1)
                act.activation(probs_t[:, j, t], turn_bank[t][:, 0:TOKENS], ACT.Copy).then_inc(turned_ready[t], 1)

            def take_h(b):
                act.wait_ge(h_turned, b + 1)
                act.activation(h_t[:, b], q_bank[:, 0:TOKENS], ACT.Identity, bias=col["ln_b"],
                               scale=col["ln_g"]).then_inc(h_ready, 1)

            def relu(b):
                act.wait_ge(mix_read, TILES * (b + 1))
                act.activation(y[:, b], pre[:, b], ACT.Relu).then_inc(relu_ready, 1)

            def take_q(b):
                act.wait_ge(q_made, b + 1)
                act.wait_ge(bq_folds_ready, 2)
                act.activation(q_t[:, b], q_bank[:, 0:TOKENS], ACT.Identity, bias=bq_wk[:]).then_inc(q_ready, 1)

            steps = {"G": take_g, "A": take_wh_wo, "C": take_w1w2, "W": take_wvp, "M": take_wqk, "E": exponentials, "V": take_values,
                     "P": take_turned, "H": take_h, "Q": take_q, "Y": relu}
            for step in ACT_ORDER:
                steps[step[0]](*map(int, step[1:]))

        @block.vector
        def _(dve):

            def take_f(_):
                dve.wait_ge(fold0_in, 16)
                dve.wait_ge(fg_made, 1)
                dve.tensor_scalar(f_all[:], q_bank[:, 0:TOKENS], col["bf"], None, ALU.add).then_inc(f_ready, 1)
                dve.wait_ge(f_ready, 1)
                dve.tensor_copy(f_high[:], f_all[:]).then_inc(f_high_ready, 1)
                dve.wait_ge(f_high_ready, 1)
                dve.scalar_tensor_tensor(out=f_parts[:], in0=f_high[:].bitcast(F32), scalar=col["low_half"], in1=f_all[:],
                                         op0=ALU.mult, op1=ALU.add).then_inc(f_parts_ready, 1)

            def split_g(_):
                dve.wait_ge(g_high_ready, 1)
                dve.wait_ge(g_ready, 1)
                dve.tensor_tensor(out=g_low[:], in0=g_all[:], in1=g_high[:].bitcast(F32),
                                  op=ALU.subtract).then_inc(g_low_ready, 1)

            def split_x(b):
                dve.wait_ge(first_in, 16)
                dve.tensor_copy(x_high[:, b], x_of(b)).then_inc(x_high_ready[b], 1)
                dve.wait_ge(x_high_ready[b], 1)
                dve.tensor_tensor(out=x_low[:, b], in0=x_of(b), in1=x_high[:, b].bitcast(F32),
                                  op=ALU.subtract).then_inc(x_low_ready[b], 1)

            def fold_norm(_):
                dve.wait_ge(fold0_in, 16)
                dve.tensor_scalar(var_eps[:], col["bn_var"], BN_EPS, None, ALU.add).then_inc(eps_added, 1)
                dve.tensor_tensor(out=centre[:], in0=col["bc"], in1=col["bn_mean"], op=ALU.subtract).then_inc(centred, 1)

            def fold_a(_):
                dve.tensor_tensor(out=both_t[:], in0=w["wc_top_t"], in1=w["wc_bottom_t"],
                                  op=ALU.add).then_inc(both_added, 1)
                dve.wait_ge(powered, 1)
                dve.tensor_tensor(out=bn_a[:], in0=power[:], in1=col["bn_scale"], op=ALU.mult).then_inc(a_ready, 1)
                dve.wait_ge(a_ready, 1)
                dve.tensor_tensor(out=gamma_a[:], in0=bn_a[:], in1=col["gamma"], op=ALU.mult).then_inc(gamma_a_ready, 1)
                dve.wait_ge(centred, 1)
                dve.scalar_tensor_tensor(out=shift[:], in0=centre[:], scalar=bn_a[:], in1=col["bn_bias"],
                                         op0=ALU.mult, op1=ALU.add).then_inc(shift_ready, 1)
                dve.wait_ge(both_added, 1)
                dve.tensor_scalar(w2_t[:], both_t[:], bn_a[:], None, ALU.mult).then_inc(w2_t_ready, 1)

            def fold_w1(_):
                dve.wait_ge(gamma_a_ready, 1)
                dve.wait_ge(w1_t_made, 1)
                dve.tensor_scalar(w1_t[:], value_bank[:, 0:C], gamma_a[:], None, ALU.mult).then_inc(w1_t_ready, 1)
                dve.wait_ge(shift_ready, 1)
                dve.scalar_tensor_tensor(out=const0_col[:], in0=value_bank[:, C:C + 1], scalar=gamma_a[:],
                                         in1=shift[:], op0=ALU.mult, op1=ALU.add).then_inc(const0_col_ready, 1)

            def split_w1w2(_):
                dve.wait_ge(w1w2_high_ready, 1)
                dve.tensor_tensor(out=w1w2_low[:], in0=fold_bank[:, 0:2 * C], in1=w1w2_high[:].bitcast(F32),
                                  op=ALU.subtract).then_inc(w1w2_low_ready, 1)

            def take_const0(_):
                dve.wait_ge(const0_made, 1)
                dve.tensor_copy(const0[:, 0], turn_bank[0][:, 0:C]).then_inc(const0_ready, 1)

            def take_const1(_):
                dve.wait_ge(const1_made, 1)
                dve.tensor_copy(const1[:, 0], fold_bank[:, 0:C]).then_inc(const1_ready, 1)

            def maxima(j):
                dve.wait_ge(scores_made, TILES * (j + 1))
                dve.tensor_reduce(neg_max[:, j], score_bank[j % 2][:].rearrange("p (t m) -> p t m", t=TILES),
                                  AX_X, ALU.max, negate=True).then_inc(max_ready, 1)

            def shift_maxima(b):
                j = IMAGES + b
                dve.wait_ge(max_ready, j + 1)
                dve.wait_ge(values_ready, j + 1)
                dve.wait_ge(bq_folds_ready, 2)
                h_wq_bk = values[:, j, :, 0, C]
                dve.scalar_tensor_tensor(out=true_neg_max[:, b], in0=neg_max[:, j], scalar=bq_bk[:], in1=h_wq_bk,
                                         op0=ALU.subtract, op1=ALU.subtract).then_inc(true_max_ready, 1)
                dve.wait_ge(true_max_ready, b + 1)
                dve.scalar_tensor_tensor(out=exp_bias[:, b], in0=true_neg_max[:, b], scalar=bq_bk[:], in1=h_wq_bk,
                                         op0=ALU.add, op1=ALU.add).then_inc(exp_bias_ready, 1)

            def last_maxima(_):
                b, j = IMAGES - 1, ATTENTIONS - 1
                h_wq_bk = values[:, j, :, 0, C]

                def maximum(t):
                    dve.wait_ge(scores_made, TILES * j + t + 1)
                    dve.tensor_reduce(neg_max[:, j, t:t + 1], scores_of(j, t), AX_X, ALU.max, negate=True).then_inc(max_ready, 1)

                def true_maximum(t):
                    dve.wait_ge(max_ready, j + t + 1)
                    dve.scalar_tensor_tensor(out=true_neg_max[:, b, t:t + 1], in0=neg_max[:, j, t:t + 1], scalar=bq_bk[:],
                                             in1=h_wq_bk[:, t:t + 1], op0=ALU.subtract, op1=ALU.subtract).then_inc(true_max_ready, 1)

                def bias(t):
                    dve.wait_ge(true_max_ready, b + t + 1)
                    dve.scalar_tensor_tensor(out=exp_bias[:, b, t:t + 1], in0=true_neg_max[:, b, t:t + 1], scalar=bq_bk[:],
                                             in1=h_wq_bk[:, t:t + 1], op0=ALU.add, op1=ALU.add).then_inc(exp_bias_ready, 1)

                dve.wait_ge(values_ready, j + 1)
                maximum(0)
                true_maximum(0)
                maximum(1)
                bias(0)
                true_maximum(1)
                bias(1)

            def take_turned(j, t):
                dve.wait_ge(turned, TILES * j + t + 1)
                dve.tensor_copy(probs_t[:, j, t], turn_bank[t][:, 0:TOKENS]).then_inc(turned_ready[t], 1)

            def take_values(j):
                dve.wait_ge(xv_made, j + 1)
                dve.wait_ge(ones_set, 1)
                if j < IMAGES:
                    made = value_bank[:].rearrange("p (t k n) -> p t k n", t=TILES, k=2)
                    taken = values[:, j, :, :, 0:C]
                else:
                    made = value_bank[:, 0:TILES * (C + 1)].rearrange("p (t n) -> p t n", t=TILES)
                    taken = values[:, j, :, 0, 0:C + 1]
                dve.tensor_copy(taken, made).then_inc(values_ready, 1)

            def take_q(b):
                dve.wait_ge(q_made, b + 1)
                dve.wait_ge(bq_folds_ready, 2)
                dve.tensor_scalar(q_t[:, b], q_bank[:, 0:TOKENS], bq_wk[:], None, ALU.add).then_inc(q_ready, 1)

            def invert(j):
                dve.wait_ge(mixed, j + 1)
                sums = mix_banks[j % 2][:, 0:TILES * VW].rearrange("p (t n) -> p t n", t=TILES)[:, :, C + 1]
                dve.reciprocal(inv_sum[:, j], sums).then_inc(inv_ready, 1)

            def take_mixed_tile(j, t):
                b, last = j % IMAGES, j >= IMAGES
                dve.scalar_tensor_tensor(out=(result if last else pre)[:, b, t], in0=mixed_tile(j, t)[:, 0:C],
                                         scalar=inv_sum[:, j, t:t + 1], in1=(y_const if last else xw2)[:, b, t],
                                         op0=ALU.mult, op1=ALU.add).then_inc(mix_read, 1)

            def take_mixed(j):
                dve.wait_ge(inv_ready, j + 1)
                if j >= IMAGES:
                    dve.wait_ge(y_const_ready, j - IMAGES + 1)
                else:
                    dve.wait_ge(xw2_ready, j + 1)
                for t in range(TILES):
                    take_mixed_tile(j, t)

            def finish(_):
                j = ATTENTIONS - 1
                dve.wait_ge(y_const_ready, IMAGES)
                for t in range(TILES):
                    dve.wait_ge(mixed, j + t + 1)
                    dve.reciprocal(inv_sum[:, j, t:t + 1], mixed_tile(j, t)[:, C + 1:C + 2]).then_inc(inv_ready, 1)
                    dve.wait_ge(inv_ready, j + t + 1)
                    take_mixed_tile(j, t)

            def relu(b):
                dve.wait_ge(mix_read, TILES * (b + 1))
                dve.tensor_scalar(y[:, b], pre[:, b], 0.0, None, ALU.max).then_inc(relu_ready, 1)

            def statistics(b, t):
                dve.wait_ge(relu_ready, b + 1)
                dve.bn_stats(stats[:, b, t], y[:, b, t]).then_inc(stats_ready, 1)

            def aggregate(b):
                for t in range(TILES):
                    dve.wait_ge(stats_ready, TILES * b + t + 1)
                    dve.bn_aggr(mean_var[:, b, t], stats[:, b, t]).then_inc(mean_ready, 1)

            def add_ln_eps(b):
                dve.wait_ge(mean_ready, TILES * (b + 1))
                dve.tensor_scalar(ln_var[:, b], mean_var[:, b, :, 1], LN_EPS, None, ALU.add).then_inc(ln_eps_added, 1)

            def normalise(b):
                dve.wait_ge(rstd_ready, b + 1)
                for t in range(TILES):
                    dve.tensor_scalar(normed[:, b, t], y[:, b, t], mean_var[:, b, t, 0:1], rstd[:, b, t:t + 1],
                                      ALU.subtract, ALU.mult).then_inc(normed_ready, 1)

            def take_h(b):
                dve.wait_ge(h_turned, b + 1)
                dve.tensor_scalar(h_t[:, b], q_bank[:, 0:TOKENS], col["ln_g"], col["ln_b"],
                                  ALU.mult, ALU.add).then_inc(h_ready, 1)

            steps = {"A": fold_norm, "F": take_f, "G": split_g, "X": split_x, "B": fold_a, "C": fold_w1, "D": split_w1w2,
                     "I": take_const0, "J": take_const1, "N": maxima, "K": last_maxima, "T": shift_maxima, "P": take_turned, "V": take_values,
                     "R": invert, "O": take_mixed, "Y": relu, "S": statistics, "M": aggregate, "E": add_ln_eps,
                     "L": normalise, "H": take_h, "Q": take_q, "Z": finish}
            for step in DVE_ORDER:
                steps[step[0]](*map(int, step[1:]))

        @block.tensor
        def _(pe):
            def warm_up(_):
                pe.matmul(score_bank[1][:], nc.const_aps.tensor(1.0, [P, P], BF16), nc.const_aps.tensor(1.0, [P, 512], BF16),
                          start=True, stop=True)

            def make_fg(_):
                pe.wait_ge(first_in, 16)
                for n, weights in enumerate((wf2, wg2)):
                    for b in range(IMAGES):
                        mm = pe.matmul((q_bank, g_bank)[n][BLOCK * b:BLOCK * (b + 1), 0:TOKENS], weights,
                                       x_t[:, b * TOKENS:(b + 1) * TOKENS], start=True, stop=True)
                    mm.then_inc(fg_made, 1)

            def fold_wh_wo(_):
                pe.wait_ge(fold0_in, 16)
                pe.matmul(fold_bank[:, 0:C + 1], w["wo"][0:CV, :], wh_t_bh, start=True, stop=True)
                pe.matmul(fold_bank[:, C:C + 1], identity, col["bo"], start=False, stop=True,
                          skip_group_check=True).then_inc(wh_wo_made, 1)

            def fold_w1(_):
                pe.wait_ge(wh_wo_ready, 1)
                pe.matmul(value_bank[:, 0:C + 1], w["wc_top"], wh_wo_t[:], start=True, stop=True).then_inc(w1_t_made, 1)

            def turn_w1w2(_):
                pe.wait_ge(w1_t_ready, 1)
                pe.transpose(fold_bank[:, 0:C], w1_t[:], identity)
                pe.wait_ge(w2_t_ready, 1)
                pe.transpose(fold_bank[:, C:2 * C], w2_t[:], identity).then_inc(w1w2_made, 1)

            def spread_const0(_):
                pe.wait_ge(const0_col_ready, 1)
                pe.matmul(turn_bank[0][:, 0:C], const0_col[:].to_broadcast([P, P]), identity,
                          start=True, stop=True).then_inc(const0_made, 1)

            def fold_wvp(_):
                pe.wait_ge(fold1_in, 16)
                pe.matmul(turn_bank[1][:, 0:C], w["wv_t"], w["wp"], start=True, stop=True).then_inc(wvp_made, 1)

            def fold_wqk(_):
                pe.wait_ge(fold1_in, 16)
                pe.matmul(score_bank[0][:, 0:C + 1], w["wq_t"], wk_t_bk, start=True, stop=True)
                pe.matmul(score_bank[0][:, C + 1:C + 2], w["wk_t"], col["bq"], start=True, stop=True)
                pe.matmul(score_bank[0][:, C + 2:C + 3], col["bq"].to_broadcast([P, P]), wk_t_bk[:, C:C + 1],
                          start=True, stop=True).then_inc(wqk_made, 1)

            def spread_const1(_):
                pe.wait_ge(w1w2_low_ready, 1)
                pe.matmul(fold_bank[:, 0:C], col["bv"].to_broadcast([P, P]), w["wp"], start=True, stop=False)
                pe.matmul(fold_bank[:, 0:C], col["bp"].to_broadcast([P, P]), identity,
                          start=False, stop=True).then_inc(const1_made, 1)

            def make_scores(j):
                if j >= 2:
                    pe.wait_ge(probs_ready, TILES * (j - 1))
                if j < IMAGES:
                    if j == 0:
                        pe.wait_ge(bq_folds_ready, 2)
                        pe.wait_ge(f_parts_ready, 1)
                        pe.wait_ge(g_high_ready, 1)
                        pe.wait_ge(g_low_ready, 1)
                    at = slice(BLOCK * j, BLOCK * (j + 1))
                    parts = [(g_high[at, :], f_parts[at, :]), (g_low[at, :], f_parts[at, :])]
                else:
                    b = j - IMAGES
                    pe.wait_ge(q_ready, b + 1)
                    parts = [(q_t[:, b], h_t[:, b])]
                for t in range(TILES):
                    for n, (queries, keys) in enumerate(parts):
                        mm = pe.matmul(scores_of(j, t), queries[:, t * P:(t + 1) * P], keys, start=(n == 0),
                                       stop=(n == len(parts) - 1))
                    mm.then_inc(scores_made, 1)

            def make_xv(j):
                if j == 0:
                    pe.wait_ge(w1w2_high_ready, 1)
                    pe.wait_ge(w1w2_low_ready, 1)
                    pe.wait_ge(const0_col_ready, 1)
                else:
                    pe.wait_ge(values_ready, j)
                if j < IMAGES:
                    pe.wait_ge(x_high_ready[j], 1)
                    pe.wait_ge(x_low_ready[j], 1)
                    parts, span = [(x_high[:, j], w1w2_high[:]), (x_high[:, j], w1w2_low[:]), (x_low[:, j], w1w2_high[:])], 2 * C
                else:
                    if j == IMAGES:
                        pe.wait_ge(wvp_ready, 1)
                        pe.wait_ge(wq_bk_ready, 1)
                    pe.wait_ge(h_ready, j - IMAGES + 1)
                    parts, span = [(h_t[:, j - IMAGES], wvp[:])], C + 1
                for t in range(TILES):
                    for n, (tokens, weights) in enumerate(parts):
                        mm = pe.matmul(value_bank[:, t * span:(t + 1) * span], tokens[:, t * P:(t + 1) * P], weights,
                                       start=(n == 0), stop=(n == len(parts) - 1))
                mm.then_inc(xv_made, 1)

            def turn(j):
                for t in range(TILES):
                    if j >= 1:
                        pe.wait_ge(turned_ready[t], j)
                    elif t == 0:
                        pe.wait_ge(const0_ready, 1)
                    else:
                        pe.wait_ge(wvp_ready, 1)
                    pe.wait_ge(probs_ready, TILES * j + t + 1)
                    for m in range(TILES):
                        mm = pe.transpose(turn_bank[t][:, m * P:(m + 1) * P], probs[:, j, t, m * P:(m + 1) * P], identity)
                    mm.then_inc(turned, 1)

            def mix(j):
                if j == 0:
                    pe.wait_ge(ones_set, 1)
                    pe.wait_ge(const1_ready, 1)
                elif j == 1:
                    pe.wait_ge(g_high_ready, 1)
                    pe.wait_ge(g_ready, 1)
                else:
                    pe.wait_ge(mix_read, TILES * (j - 1))
                pe.wait_ge(values_ready, j + 1)
                for t in range(TILES):
                    if j == ATTENTIONS - 1 and t > 0:
                        pe.wait_ge(mix_read, TILES * j)
                    pe.wait_ge(turned_ready[t], j + 1)
                    for m in range(TILES):
                        mm = pe.matmul(mixed_tile(j, t), probs_t[:, j, t, m * P:(m + 1) * P],
                                       values[:, j, m, 0, :], start=(m == 0), stop=(m == TILES - 1))
                    if j == ATTENTIONS - 1 or t == TILES - 1:
                        mm.then_inc(mixed, 1)

            def turn_h(b):
                if b == 0:
                    pe.wait_ge(f_ready, 1)
                else:
                    pe.wait_ge(q_ready, b)
                for t in range(TILES):
                    pe.wait_ge(normed_ready, TILES * b + t + 1)
                    mm = pe.transpose(q_bank[:, t * P:(t + 1) * P], normed[:, b, t], identity)
                mm.then_inc(h_turned, 1)

            def make_q(b):
                if b == 0:
                    pe.wait_ge(wqk_ready, 1)
                pe.wait_ge(h_ready, b + 1)
                pe.matmul(q_bank[:, 0:TOKENS], wqk[:], h_t[:, b], start=True, stop=True).then_inc(q_made, 1)

            steps = {"W": warm_up, "F": make_fg, "A": fold_wh_wo, "B": fold_w1, "C": turn_w1w2, "D": spread_const0,
                     "K": fold_wvp, "G": fold_wqk, "J": spread_const1, "S": make_scores, "X": make_xv, "V": make_xv, "T": turn,
                     "M": mix, "H": turn_h, "Q": make_q}
            for step in PE_ORDER:
                steps[step[0]](*map(int, step[1:]))


OUT_SHAPE = (IMAGES, 16, 16, C)


def kernel(**inputs):
    import numpy as np
    import concourse.bacc as bacc
    from concourse.bass_utils import run_bass_kernel_spmd

    given = {n.removeprefix("L0_conv_").removeprefix("L1_conv_"): np.asarray(a) for n, a in inputs.items()}

    def padded(a, columns):
        out = np.zeros((P, columns), np.float32)
        out[:a.shape[0], :a.shape[1]] = a
        return out

    def column(name):
        if name == "low_half":
            return -(np.arange(P) % BLOCK >= CK).astype(np.float32)[:, None]
        a = given[name].reshape(-1)
        if name in ("bf", "bg"):
            a = np.tile(a, P // CK)
        if name == "gamma":
            a = np.tile(a, P)
        return padded(a[:, None], 1)

    wc = given["wc"]
    blocks = {
        "wo": given["wo"], "wh_t": given["wh"].T, "bh": given["bh"][:, None], "wc_top": wc[:C], "wc_top_t": wc[:C].T,
        "wc_bottom_t": wc[C:].T, "identity": np.eye(C),
        "wv_t": given["Wv"].T, "wp": given["Wp"], "wq_t": given["Wq"].T, "wk_t": given["Wk"].T,
    }
    arrays = {
        "first": np.concatenate([given["x"].reshape(IMAGES * TOKENS, C).T]
                                + [given[n] for n in ("wf", "wf", "wg", "wg")], axis=1),
        "fold0": np.concatenate([padded(blocks[n], blocks[n].shape[1]) for n in FOLD0]
                                + [column(n) for n in COL_NAMES], axis=1),
        "fold1": np.concatenate([blocks[n] for n in FOLD1] + [given["bk"][:, None]], axis=1),
    }
    arrays = {n: np.ascontiguousarray(a) for n, a in arrays.items()}
    nc = bacc.Bacc("TRN2", target_bir_lowering=False, num_devices=1)
    args = [nc.dram_tensor(n, a.shape, F32, kind="ExternalInput").ap() for n, a in arrays.items()]
    out = nc.dram_tensor("out", (IMAGES, TOKENS, C), F32, kind="ExternalOutput").ap()
    attention_blocks(nc, *args, out)
    got = run_bass_kernel_spmd(nc, [arrays], core_ids=[0])
    return got.results[0]["out"].reshape(OUT_SHAPE)
```
